# Optimizing a Trainium2 kernel written in Bass

```python
import numpy as np
import jax
import jax.numpy as jnp

def _softmax(x, axis=-1):
    return jax.nn.softmax(x, axis=axis)

def _gelu(x):
    return jax.nn.gelu(x, approximate=True)

def _silu(x):
    return jax.nn.silu(x)

def _sigmoid(x):
    return jax.nn.sigmoid(x)

def _layernorm(x, axis=-1, eps=1e-05):
    m = jnp.mean(x, axis=axis, keepdims=True)
    v = jnp.var(x, axis=axis, keepdims=True)
    return (x - m) / jnp.sqrt(v + eps)

def _scatter_add(tgt, idx, src, axis=0):
    return tgt.at[idx].add(src)

def _segment_sum(src, seg, n):
    return jax.ops.segment_sum(src, seg, n)
kernel_name = 'mk_flamingo_gated_d2_seqx_r4_cddc26'

def setup_inputs(seed: int=0):
    np.random.seed(seed)
    _w = jnp.asarray

    def _rec_inputs():
        import jax
        import jax.numpy as jnp
        _rk = jax.random.key(seed)
        x = -0.0002928 + 1 * jax.random.normal(jax.random.fold_in(_rk, 1), (8, 512, 256), jnp.float32)
        _lenS = 512 - jax.random.randint(jax.random.fold_in(_rk, 7), (8,), 0, max(1, 512 // 4) + 1, jnp.int32)
        _lenS2 = 512 - jax.random.randint(jax.random.fold_in(_rk, 8), (8,), 0, max(1, 512 // 4) + 1, jnp.int32)
        _ctx_1024P = jax.random.normal(jax.random.fold_in(_rk, 11), (8, 16, 256), jnp.float32)
        _ctx_1024c = jax.random.dirichlet(jax.random.fold_in(_rk, 511), 0.3 * jnp.ones((16,), jnp.float32), (8, 512))
        _ctx_1024t = jnp.einsum('bsk,bkd->bsd', _ctx_1024c, _ctx_1024P)
        _ctx_1024t = _ctx_1024t * jax.lax.rsqrt(jnp.mean(jnp.square(_ctx_1024t)) + 1e-12) * 0.953939
        ctx_1024 = -1.39393e-06 + 0.999914 * (_ctx_1024t + 0.3 * jax.random.normal(jax.random.fold_in(_rk, 611), (8, 512, 256), jnp.float32))
        _validS = jnp.arange(512)[None, :] < _lenS[:, None]
        _validS2 = jnp.arange(512)[None, :] < _lenS2[:, None]
        _causal = jnp.tril(jnp.ones((512, 512), dtype=bool))
        mask_BxS2_bf1 = jnp.ones((8, 512), dtype=bool)
        _g = jax.random.normal(jax.random.fold_in(_rk, 9001), (2, 2), jnp.float32)
        _g = jnp.sign(_g) * jnp.maximum(jnp.abs(_g), 1.0) + (_g == 0) * 1.0
        g_xattn = _g[0]
        g_ffn = _g[1]
        return (x, ctx_1024, mask_BxS2_bf1, g_xattn, g_ffn)
    x, ctx_1024, mask_BxS2_bf1, g_xattn, g_ffn = _rec_inputs()

    def _L0_xattn_setup():
        import jax, jax.numpy as jnp
        import numpy as np
        N_HEADS = 16
        D_MODEL = 256
        HEAD_DIM = D_MODEL // N_HEADS
        MASK_FILL = -100000000.0

        def _split_heads(x):
            B, S, _ = x.shape
            return x.reshape(B, S, N_HEADS, HEAD_DIM).transpose(0, 2, 1, 3)
        key = jax.random.key(seed)
        ks = jax.random.split(key, 12)
        B, L, P = (2, 512, 512)
        s = 1.0 / np.sqrt(D_MODEL).astype(np.float32)
        inp = {'q': jax.random.normal(ks[0], (B, L, D_MODEL), dtype=jnp.float32), 'k': jax.random.normal(ks[1], (B, P, D_MODEL), dtype=jnp.float32), 'v': jax.random.normal(ks[2], (B, P, D_MODEL), dtype=jnp.float32), 'attention_mask': jnp.ones((B, P), dtype=bool), 'Wq': jax.random.normal(ks[3], (D_MODEL, D_MODEL), dtype=jnp.float32) * s, 'bq': jnp.zeros((D_MODEL,), dtype=jnp.float32), 'Wk': jax.random.normal(ks[4], (D_MODEL, D_MODEL), dtype=jnp.float32) * s, 'bk': jnp.zeros((D_MODEL,), dtype=jnp.float32), 'Wv': jax.random.normal(ks[5], (D_MODEL, D_MODEL), dtype=jnp.float32) * s, 'bv': jnp.zeros((D_MODEL,), dtype=jnp.float32), 'Wo': jax.random.normal(ks[6], (D_MODEL, D_MODEL), dtype=jnp.float32) * s, 'bo': jnp.zeros((D_MODEL,), dtype=jnp.float32)}
        return inp
    _L0_xattn_all = _L0_xattn_setup()
    _L0_xattn_in = {k: v for k, v in _L0_xattn_all.items() if k in ('Wq', 'bq', 'Wk', 'bk', 'Wv', 'bv', 'Wo', 'bo')}
    del _L0_xattn_all

    def _L0_ffn_setup():
        import jax, jax.numpy as jnp
        import numpy as np
        EPS = 1e-05
        TOP_K = 2

        def _rmsnorm(x, w):
            xf = x.astype(jnp.float32)
            rms = jax.lax.rsqrt(jnp.mean(xf * xf, axis=-1, keepdims=True) + EPS)
            return (xf * rms).astype(x.dtype) * w

        def _attention(x, wq, wk, wv, wo, num_heads=16):
            B, S, H = x.shape
            D = H // num_heads
            q = (x @ wq.T).reshape(B, S, num_heads, D)
            k = (x @ wk.T).reshape(B, S, num_heads, D)
            v = (x @ wv.T).reshape(B, S, num_heads, D)
            scale = 1.0 / jnp.sqrt(jnp.float32(D)).astype(x.dtype)
            scores = jnp.einsum('bqhd,bkhd->bhqk', q, k) * scale
            probs = jax.nn.softmax(scores, axis=-1)
            out = jnp.einsum('bhqk,bkhd->bqhd', probs, v).reshape(B, S, H)
            return out @ wo.T

        def _moe(x, gate_w, w1, w2, w3):
            B, S, H = x.shape
            xf = x.reshape(-1, H)
            logits = xf @ gate_w.T
            rw, sel = jax.lax.top_k(logits, TOP_K)
            rw = jax.nn.softmax(rw.astype(jnp.float32), axis=-1).astype(x.dtype)
            E = gate_w.shape[0]
            out = jnp.zeros_like(xf)
            for e in range(E):
                we = jnp.sum(jnp.where(sel == e, rw, 0.0), axis=-1)
                h = jax.nn.silu(xf @ w1[e].T) * (xf @ w3[e].T)
                out = out + h @ w2[e].T * we[:, None]
            return out.reshape(B, S, H)
        key = jax.random.key(seed)
        ks = jax.random.split(key, 10)
        H, I, E, NH = (256, 512, 8, 16)
        B, S = (2, 512)
        s = 0.02
        return {'x': jax.random.normal(ks[0], (B, S, H), jnp.float32), 'ln1_w': jnp.ones((H,), jnp.float32), 'ln2_w': jnp.ones((H,), jnp.float32), 'wq': jax.random.normal(ks[1], (H, H), jnp.float32) * s, 'wk': jax.random.normal(ks[2], (H, H), jnp.float32) * s, 'wv': jax.random.normal(ks[3], (H, H), jnp.float32) * s, 'wo': jax.random.normal(ks[4], (H, H), jnp.float32) * s, 'gate_w': jax.random.normal(ks[5], (E, H), jnp.float32) * s, 'w1': jax.random.normal(ks[6], (E, I, H), jnp.float32) * s, 'w2': jax.random.normal(ks[7], (E, H, I), jnp.float32) * s, 'w3': jax.random.normal(ks[8], (E, I, H), jnp.float32) * s}
    _L0_ffn_all = _L0_ffn_setup()
    _L0_ffn_in = {k: v for k, v in _L0_ffn_all.items() if k in ('ln1_w', 'ln2_w', 'wq', 'wk', 'wv', 'wo', 'gate_w', 'w1', 'w2', 'w3')}
    del _L0_ffn_all

    def _L1_xattn_setup():
        import jax, jax.numpy as jnp
        import numpy as np
        DIM = 256
        NUM_HEADS = 16
        HEAD_DIM = DIM // NUM_HEADS
        key = jax.random.key(seed)
        ks = jax.random.split(key, 11)
        B, N, C = (2, 512, DIM)
        s = 1.0 / np.sqrt(C)
        inp = {'q': jax.random.normal(ks[0], (B, N, C), jnp.float32), 'k': jax.random.normal(ks[1], (B, N, C), jnp.float32), 'v': jax.random.normal(ks[2], (B, N, C), jnp.float32), 'Wq': jax.random.normal(ks[3], (C, C), jnp.float32) * s, 'bq': jnp.zeros((C,), jnp.float32), 'Wk': jax.random.normal(ks[4], (C, C), jnp.float32) * s, 'bk': jnp.zeros((C,), jnp.float32), 'Wv': jax.random.normal(ks[5], (C, C), jnp.float32) * s, 'bv': jnp.zeros((C,), jnp.float32), 'Wo': jax.random.normal(ks[6], (C, C), jnp.float32) * s, 'bo': jnp.zeros((C,), jnp.float32)}
        return inp
    _L1_xattn_all = _L1_xattn_setup()
    _L1_xattn_in = {k: v for k, v in _L1_xattn_all.items() if k in ('Wq', 'bq', 'Wk', 'bk', 'Wv', 'bv', 'Wo', 'bo')}
    del _L1_xattn_all

    def _L1_ffn_setup():
        import jax, jax.numpy as jnp
        import numpy as np
        E = 8
        K = 2
        R = 64
        ALPHA = 128.0
        SCALING = ALPHA / R
        key = jax.random.key(seed)
        k0, k1, k2, k3 = jax.random.split(key, 4)
        B, S, D = (4, 1024, 256)
        x = jax.random.normal(k0, (B, S, D), jnp.float32)
        Wg = jax.random.normal(k1, (E, D), jnp.float32) * 0.02
        bg = jnp.zeros((E,), jnp.float32)
        W1 = jax.random.normal(k2, (E, R, D), jnp.float32) * (1.0 / np.sqrt(D))
        W2 = jax.random.normal(k3, (E, D, R), jnp.float32) * 0.02
        return {'x': x, 'Wg': Wg, 'bg': bg, 'W1': W1, 'W2': W2}
    _L1_ffn_all = _L1_ffn_setup()
    _L1_ffn_in = {k: v for k, v in _L1_ffn_all.items() if k in ('Wg', 'bg', 'W1', 'W2')}
    del _L1_ffn_all
    return {'x': x, 'ctx_1024': ctx_1024, 'mask_BxS2_bf1': mask_BxS2_bf1, 'g_xattn': g_xattn, 'g_ffn': g_ffn, 'L0_xattn_Wq': _L0_xattn_in['Wq'], 'L0_xattn_bq': _L0_xattn_in['bq'], 'L0_xattn_Wk': _L0_xattn_in['Wk'], 'L0_xattn_bk': _L0_xattn_in['bk'], 'L0_xattn_Wv': _L0_xattn_in['Wv'], 'L0_xattn_bv': _L0_xattn_in['bv'], 'L0_xattn_Wo': _L0_xattn_in['Wo'], 'L0_xattn_bo': _L0_xattn_in['bo'], 'L0_ffn_ln1_w': _L0_ffn_in['ln1_w'], 'L0_ffn_ln2_w': _L0_ffn_in['ln2_w'], 'L0_ffn_wq': _L0_ffn_in['wq'], 'L0_ffn_wk': _L0_ffn_in['wk'], 'L0_ffn_wv': _L0_ffn_in['wv'], 'L0_ffn_wo': _L0_ffn_in['wo'], 'L0_ffn_gate_w': _L0_ffn_in['gate_w'], 'L0_ffn_w1': _L0_ffn_in['w1'], 'L0_ffn_w2': _L0_ffn_in['w2'], 'L0_ffn_w3': _L0_ffn_in['w3'], 'L1_xattn_Wq': _L1_xattn_in['Wq'], 'L1_xattn_bq': _L1_xattn_in['bq'], 'L1_xattn_Wk': _L1_xattn_in['Wk'], 'L1_xattn_bk': _L1_xattn_in['bk'], 'L1_xattn_Wv': _L1_xattn_in['Wv'], 'L1_xattn_bv': _L1_xattn_in['bv'], 'L1_xattn_Wo': _L1_xattn_in['Wo'], 'L1_xattn_bo': _L1_xattn_in['bo'], 'L1_ffn_Wg': _L1_ffn_in['Wg'], 'L1_ffn_bg': _L1_ffn_in['bg'], 'L1_ffn_W1': _L1_ffn_in['W1'], 'L1_ffn_W2': _L1_ffn_in['W2']}

def reference(x, ctx_1024, mask_BxS2_bf1, g_xattn, g_ffn, L0_xattn_Wq, L0_xattn_bq, L0_xattn_Wk, L0_xattn_bk, L0_xattn_Wv, L0_xattn_bv, L0_xattn_Wo, L0_xattn_bo, L0_ffn_ln1_w, L0_ffn_ln2_w, L0_ffn_wq, L0_ffn_wk, L0_ffn_wv, L0_ffn_wo, L0_ffn_gate_w, L0_ffn_w1, L0_ffn_w2, L0_ffn_w3, L1_xattn_Wq, L1_xattn_bq, L1_xattn_Wk, L1_xattn_bk, L1_xattn_Wv, L1_xattn_bv, L1_xattn_Wo, L1_xattn_bo, L1_ffn_Wg, L1_ffn_bg, L1_ffn_W1, L1_ffn_W2):
    import jax
    import jax.numpy as jnp

    def _L0_xattn_ref(q, k, v, attention_mask, Wq, bq, Wk, bk, Wv, bv, Wo, bo):
        import jax, jax.numpy as jnp
        import numpy as np
        N_HEADS = 16
        D_MODEL = 256
        HEAD_DIM = D_MODEL // N_HEADS
        MASK_FILL = -100000000.0

        def _split_heads(x):
            B, S, _ = x.shape
            return x.reshape(B, S, N_HEADS, HEAD_DIM).transpose(0, 2, 1, 3)
        qm = _split_heads(q @ Wq.T + bq)
        km = _split_heads(k @ Wk.T + bk)
        vm = _split_heads(v @ Wv.T + bv)
        scores = jnp.einsum('bnlh,bnph->bnlp', qm, km) / np.sqrt(HEAD_DIM).astype(np.float32)
        mask = attention_mask[:, None, None, :]
        scores = jnp.where(mask, scores, MASK_FILL)
        attn = jax.nn.softmax(scores, axis=-1)
        out = jnp.einsum('bnlp,bnph->bnlh', attn, vm)
        B, _, L, _ = out.shape
        out = out.transpose(0, 2, 1, 3).reshape(B, L, D_MODEL)
        return out @ Wo.T + bo

    def _L0_ffn_ref(x, ln1_w, ln2_w, wq, wk, wv, wo, gate_w, w1, w2, w3):
        import jax, jax.numpy as jnp
        import numpy as np
        EPS = 1e-05
        TOP_K = 2

        def _rmsnorm(x, w):
            xf = x.astype(jnp.float32)
            rms = jax.lax.rsqrt(jnp.mean(xf * xf, axis=-1, keepdims=True) + EPS)
            return (xf * rms).astype(x.dtype) * w

        def _attention(x, wq, wk, wv, wo, num_heads=16):
            B, S, H = x.shape
            D = H // num_heads
            q = (x @ wq.T).reshape(B, S, num_heads, D)
            k = (x @ wk.T).reshape(B, S, num_heads, D)
            v = (x @ wv.T).reshape(B, S, num_heads, D)
            scale = 1.0 / jnp.sqrt(jnp.float32(D)).astype(x.dtype)
            scores = jnp.einsum('bqhd,bkhd->bhqk', q, k) * scale
            probs = jax.nn.softmax(scores, axis=-1)
            out = jnp.einsum('bhqk,bkhd->bqhd', probs, v).reshape(B, S, H)
            return out @ wo.T

        def _moe(x, gate_w, w1, w2, w3):
            B, S, H = x.shape
            xf = x.reshape(-1, H)
            logits = xf @ gate_w.T
            rw, sel = jax.lax.top_k(logits, TOP_K)
            rw = jax.nn.softmax(rw.astype(jnp.float32), axis=-1).astype(x.dtype)
            E = gate_w.shape[0]
            out = jnp.zeros_like(xf)
            for e in range(E):
                we = jnp.sum(jnp.where(sel == e, rw, 0.0), axis=-1)
                h = jax.nn.silu(xf @ w1[e].T) * (xf @ w3[e].T)
                out = out + h @ w2[e].T * we[:, None]
            return out.reshape(B, S, H)
        h = x + _attention(_rmsnorm(x, ln1_w), wq, wk, wv, wo)
        h = h + _moe(_rmsnorm(h, ln2_w), gate_w, w1, w2, w3)
        return h

    def _L1_xattn_ref(q, k, v, Wq, bq, Wk, bk, Wv, bv, Wo, bo):
        import jax, jax.numpy as jnp
        import numpy as np
        DIM = 256
        NUM_HEADS = 16
        HEAD_DIM = DIM // NUM_HEADS
        B, Nq, C = q.shape
        Nkv = k.shape[1]
        H, D = (NUM_HEADS, HEAD_DIM)
        qh = (q @ Wq.T + bq).reshape(B, Nq, H, D).transpose(0, 2, 1, 3)
        kh = (k @ Wk.T + bk).reshape(B, Nkv, H, D).transpose(0, 2, 1, 3)
        vh = (v @ Wv.T + bv).reshape(B, Nkv, H, D).transpose(0, 2, 1, 3)
        scale = D ** (-0.5)
        attn = jax.nn.softmax(jnp.einsum('bhqd,bhkd->bhqk', qh, kh) * scale, axis=-1)
        out = jnp.einsum('bhqk,bhkd->bhqd', attn, vh)
        out = out.transpose(0, 2, 1, 3).reshape(B, Nq, C)
        return out @ Wo.T + bo

    def _L1_ffn_ref(x, Wg, bg, W1, W2):
        import jax, jax.numpy as jnp
        import numpy as np
        E = 8
        K = 2
        R = 64
        ALPHA = 128.0
        SCALING = ALPHA / R
        orig_shape = x.shape
        D = orig_shape[-1]
        xf = x.reshape(-1, D)
        logits = xf @ Wg.T + bg
        top_gates, top_idx = jax.lax.top_k(logits, K)
        top_gates = jax.nn.softmax(top_gates, axis=-1)
        h = jax.nn.gelu(jnp.einsum('nd,erd->enr', xf, W1), approximate=False)
        eout = SCALING * jnp.einsum('enr,edr->ned', h, W2)
        sel = jnp.take_along_axis(eout, top_idx[:, :, None], axis=1)
        out = jnp.sum(top_gates[:, :, None] * sel, axis=1)
        return out.reshape(orig_shape)
    x = x + jnp.tanh(g_xattn[0]) * _L0_xattn_ref(_layernorm(x, axis=-1), ctx_1024, ctx_1024, mask_BxS2_bf1, L0_xattn_Wq, L0_xattn_bq, L0_xattn_Wk, L0_xattn_bk, L0_xattn_Wv, L0_xattn_bv, L0_xattn_Wo, L0_xattn_bo)
    x = x + jnp.tanh(g_ffn[0]) * _L0_ffn_ref(_layernorm(x, axis=-1), L0_ffn_ln1_w, L0_ffn_ln2_w, L0_ffn_wq, L0_ffn_wk, L0_ffn_wv, L0_ffn_wo, L0_ffn_gate_w, L0_ffn_w1, L0_ffn_w2, L0_ffn_w3)
    x = x + jnp.tanh(g_xattn[1]) * _L1_xattn_ref(_layernorm(x, axis=-1), ctx_1024, ctx_1024, L1_xattn_Wq, L1_xattn_bq, L1_xattn_Wk, L1_xattn_bk, L1_xattn_Wv, L1_xattn_bv, L1_xattn_Wo, L1_xattn_bo)
    x = x + jnp.tanh(g_ffn[1]) * _L1_ffn_ref(_layernorm(x, axis=-1), L1_ffn_Wg, L1_ffn_bg, L1_ffn_W1, L1_ffn_W2)
    return x

_drawn_inputs = setup_inputs


def setup_inputs(seed=0):
    import zlib

    import numpy as np

    out = dict(_drawn_inputs(seed))
    spreads = {'g_ffn': (-1.0, 0.2),
     'L0_xattn_bq': (0.0, 0.1),
     'L0_xattn_bk': (0.0, 0.8),
     'L0_xattn_bv': (0.0, 0.1),
     'L0_xattn_bo': (0.0, 0.1),
     'L0_ffn_ln1_w': (1.0, 0.2),
     'L0_ffn_ln2_w': (1.0, 0.2),
     'L1_xattn_bq': (0.0, 0.1),
     'L1_xattn_bk': (0.0, 0.8),
     'L1_xattn_bv': (0.0, 0.1),
     'L1_xattn_bo': (0.0, 0.1),
     'L1_ffn_bg': (0.0, 0.1)}
    factors = {'L0_ffn_wq': 6.568, 'L0_ffn_wk': 6.039}
    for name, (base, spread) in spreads.items():
        noise = np.random.default_rng([zlib.crc32(name.encode()), seed]).standard_normal(out[name].shape)
        drawn = base * np.exp(spread * noise) if base else spread * noise
        out[name] = jnp.asarray(drawn.astype(out[name].dtype))
    for name, factor in factors.items():
        out[name] = (out[name] * factor).astype(out[name].dtype)
    return out
```

```python
from contextlib import ExitStack

import concourse.bass as bass
from concourse import mybir

P = 128
F32 = mybir.dt.float32
F32R = mybir.dt.float32r
U8 = mybir.dt.uint8
U32 = mybir.dt.uint32
I32 = mybir.dt.int32
ALU = mybir.AluOpType
ACT = mybir.ActivationFunctionType
AX = mybir.AxisListType

B, S, D = 8, 512, 256
H, HD = 16, 16
NT = S // P
NC = D // P
GH = 4
NG = H // GH
VW = 32
EPS = 1e-5
SCALE = float(HD) ** -0.5
MASKED = -1e8 / SCALE
RSQRT_SEED = 0x5F3759DF
ONE_ROW = 64
MAX_ROW = 126


def after(eng, sem, count):
    if not isinstance(count, int) or count > 0:
        eng.wait_ge(sem, count)


def hold(eng, sem, count):
    if not isinstance(count, int) or count > 0:
        eng.wait_ge(sem, count)
        eng.nop(nofuse=True)


def emit_rsqrt(dve, step, out, val, tmp):
    step(dve.tensor_scalar(tmp.bitcast(U32), val.bitcast(U32), 1, None, ALU.logical_shift_right))
    step(dve.tensor_scalar(out.bitcast(I32), tmp.bitcast(I32), -1.0, float(RSQRT_SEED), ALU.mult, ALU.add))
    for _ in range(3):
        step(dve.tensor_tensor(tmp, out, out, ALU.mult))
        step(dve.scalar_tensor_tensor(tmp, tmp, -0.5, val, ALU.mult, ALU.mult))
        step(dve.scalar_tensor_tensor(out, tmp, 1.5, out, ALU.add, ALU.mult))


def piece_table(cross):
    table = [
        ((0, 1), "N", -1), ((0, 2), "O", -3),
        ((1, 0), "T", 2), ((1, 0), "T", 3), ((1, 1), "N", 0), ((1, 1), "C", 2), ((1, 2), "O", -2), ((1, 2), "C", 3),
        ((1, 3), "Q", 2), ((1, 3), "K", 2),
        ((2, 0), "Q", 3), ((2, 0), "K", 3), ((2, 1), "N", 1), ((2, 2), "O", -1), ((2, 3), "V", 2), ((2, 3), "V", 3),
        ((3, 0), "OT", -2), ((3, 0), "OT", -1), ((3, 1), "Y", -2), ((3, 1), "Y", -1), ((3, 2), "N", 2), ((3, 3), "O", 0),
    ]
    if not cross:
        table = [t for t in table if t[1] != "C"]
    return [(at, kind, off, i % 2) for i, (at, kind, off) in enumerate(table)]


PER = {"T": 2, "C": 2, "Q": 2, "K": 2, "V": 2, "OT": 2, "Y": 2, "N": NG, "O": NG}
PREP = ("T", "C", "Q", "K", "V")


def build_attention(nc, tag, cfg):
    cross, masked = cfg["ctx"] is not None, cfg["mask"] is not None
    src, ctx_d, res_d, out_d = cfg["x"], cfg["ctx"], cfg["res"], cfg["out"]
    table = piece_table(cross)

    with ExitStack() as stack:
        def sb(name, shape, dt=F32):
            return stack.enter_context(nc.sbuf_tensor(f"{tag}_{name}", shape, dt))

        def ps(name, shape):
            return stack.enter_context(nc.psum_tensor(f"{tag}_{name}", shape, F32))

        def sem(name):
            return stack.enter_context(nc.semaphore(f"{tag}_{name}"))

        parts = nc.dram_tensor(f"{tag}_parts", [B, 2, 2, D, S], F32)
        fill = nc.dram_tensor(f"{tag}_fill", [B, 2, S], F32) if masked else None

        ident = sb("ident", [P, P])
        w_raw = sb("w_raw", [P, 4, NC, D])
        w_t = sb("w_t", [P, 4, NC, D])
        bias_col = sb("bias_col", [P, 2, NC])
        bias_row = sb("bias_row", [P, 2, D])
        gate = sb("gate", [P, 1])
        x_in = sb("x_in", [P, NT, D])
        c_in = sb("c_in", [P, NT, D]) if cross else None
        stats = sb("stats", [P, NT, 6])
        mean_var = sb("mean_var", [P, NT, 2])
        small = sb("small", [P, 6, NT])
        x_norm = sb("x_norm", [P, NT, D])
        h0 = None if cross else sb("h0", [P, NT, D])
        x_t = sb("x_t", [P, NC, S])
        c_t = sb("c_t", [P, NC, S]) if cross else x_t
        qk_full = sb("qk_full", [P, 2, NC, S])
        qk_parts = sb("qk_parts", [P, 2, 2, NC, S], F32R)
        q_stack = sb("q_stack", [P, H, S], F32R)
        k_stack = sb("k_stack", [P, H, S], F32R)
        v_new = sb("v_new", [P, NT, D])
        v_aug = sb("v_aug", [P, NT, H, VW])
        probs = sb("probs", [P, NT, GH, S])
        neg_max = sb("neg_max", [P, NT, GH])
        max_parts = sb("max_parts", [P, NT, 2, GH], F32R)
        max_rows = sb("max_rows", [2 * GH, S], F32R)
        o_raw = sb("o_raw", [P, S])
        rec = sb("rec", [P, NT, GH])
        o_tok = sb("o_tok", [P, NT, D])
        o_t = sb("o_t", [P, NC, S])
        res = sb("res", [P, NT, D])
        y_tmp = sb("y_tmp", [P, 2, D])
        y_out = sb("y_out", [P, NT, D])
        mask_b = sb("mask_b", [P, S], U8) if masked else None
        mask_r = sb("mask_r", [B, S], U8) if masked else None
        fill_f = sb("fill_f", [B, S]) if masked else None
        fill_p = sb("fill_p", [B, 2, S], F32R) if masked else None

        ps_max = ps("ps_max", [P, 2, S])
        ps_exp = ps("ps_exp", [P, 2, S])
        ps_pv = ps("ps_pv", [P, 2, S])
        ps_x = ps("ps_x", [P, 2, S])

        w_loaded, ident_made, w_turned, w_taken, gate_made = (sem(n) for n in (
            "w_loaded", "ident_made", "w_turned", "w_taken", "gate_made"))
        fill_chain, fill_stored, rows_set, v_set = (sem(n) for n in ("fill_chain", "fill_stored", "rows_set", "v_set"))
        x_loaded, c_loaded, res_loaded, y_stored, h0_stored = (sem(n) for n in (
            "x_loaded", "c_loaded", "res_loaded", "y_stored", "h0_stored"))
        parts_stored = sem("parts_stored")
        stack_loaded = [sem(f"stack_loaded{g}") for g in range(NG)]
        max_loaded = [sem(f"max_loaded{g}") for g in range(NG)]
        dve_chain = sem("dve_chain")
        stats_made, x_normed, h0_made = sem("stats_made"), sem("x_normed"), sem("h0_made")
        qk_scored, maxed, max_split = sem("qk_scored"), sem("maxed"), sem("max_split")
        kq_scored, exped, pv_done, pv_taken = sem("kq_scored"), sem("exped"), sem("pv_done"), sem("pv_taken")
        low_made, v_copied = sem("low_made"), sem("v_copied")
        made = {k: sem(f"made_{k}") for k in PER}
        taken = {k: sem(f"taken_{k}") for k in PER}
        done_y, rec_made, max_high = sem("done_y"), sem("rec_made"), sem("max_high")

        W_DMAS = 4 + (1 if not cross else 5) + (1 if masked else 0)
        NEWTON = 11
        CHAIN = (3 + NEWTON) if cross else (3 + NEWTON + 3 + NEWTON + 1)
        K_BY_DVE = masked

        def has(unit, at, kind, off):
            if kind in PREP:
                return unit in ("first", "mid")
            if unit == "first":
                return kind in ("N", "O") and off >= 0
            if unit == "tail":
                return kind in ("OT", "Y") or off < 0
            return True

        def pieces(unit, s, kt):
            return [(kind, off, bank) for at, kind, off, bank in table if at == (s, kt) and has(unit, at, kind, off)]

        def number(kind, off, b):
            return PER[kind] * b + off

        block = stack.enter_context(nc.Block())

        @block.sync
        def _(sp):
            def load_x(b):
                after(sp, x_normed, NT * b)
                if not cross:
                    after(sp, h0_made, NT * b)
                sp.dma_start(x_in[:, :, :], src[b].rearrange("(t p) d -> p t d", p=P)).then_inc(x_loaded, 16)
                if cross:
                    hold(sp, made["C"], 2 * b)
                    if masked:
                        hold(sp, taken["K"], 2 * b)
                        sp.dma_start(mask_b[:, :], cfg["mask"][bass.ds(b, 1), :].broadcast_to([P, S])).then_inc(c_loaded, 16)
                    sp.dma_start(c_in[:, :, :], ctx_d[b].rearrange("(t p) d -> p t d", p=P)).then_inc(c_loaded, 16)

            def store_h0(b):
                sp.wait_ge(h0_made, NT * b + NT)
                sp.dma_start(res_d[b].rearrange("(t p) d -> p t d", p=P), h0[:, :, :]).then_inc(h0_stored, 16)

            def store_parts(b):
                sp.wait_ge(low_made, 4 * b + 4)
                for op in range(2):
                    for part in range(2):
                        sp.dma_start(parts[b, op, part].rearrange("(g p) c -> p g c", p=P),
                                     qk_parts[:, op, part].bitcast(F32)).then_inc(parts_stored, 16)

            def load_stack(b, g):
                hold(sp, kq_scored, 16 * (NG * (b - 1) + g + 1))
                sp.wait_ge(parts_stored, 64 * (b + 1))
                heads = slice(GH * g, GH * g + GH)
                for op, dst, order in ((0, q_stack, (0, 0, 1, 1)), (1, k_stack, (0, 1, 0, 1))):
                    for row, part in enumerate(order):
                        sp.dma_start(dst[HD * row:HD * row + HD, heads, :].bitcast(F32),
                                     parts[b, op, part, 64 * g:64 * g + 64, :].rearrange("(h d) c -> d h c", d=HD)
                                     ).then_inc(stack_loaded[g], 16)
                if masked:
                    sp.dma_start(k_stack[ONE_ROW:ONE_ROW + 2, heads, :].bitcast(F32),
                                 fill[b].rearrange("r (o c) -> r o c", o=1).broadcast_to([2, GH, S])
                                 ).then_inc(stack_loaded[g], 16)

            def load_max(b, s):
                g = (s - 1) % NG
                sp.wait_ge(taken["N"], NG * b + s)
                for part in range(2):
                    sp.dma_start(q_stack[MAX_ROW + part:MAX_ROW + part + 1, GH * g:GH * g + GH, :].bitcast(F32),
                                 max_rows[GH * part:GH * part + GH, :].bitcast(F32)).then_inc(max_loaded[g], 16)

            def load_res(b):
                if not cross:
                    hold(sp, h0_stored, 16 * (b + 1))
                after(sp, done_y, 2 * b)
                sp.dma_start(res[:, :, :], res_d[b].rearrange("(t p) d -> p t d", p=P)).then_inc(res_loaded, 16)

            def store_y(b):
                sp.wait_ge(done_y, 2 * b + 2)
                sp.dma_start(out_d[b].rearrange("(t p) d -> p t d", p=P), y_out[:, :, :]).then_inc(y_stored, 16)

            def unit(b, kind):
                if kind in ("first", "mid"):
                    load_x(b + 1)
                for s in range(NG):
                    if kind in ("mid", "last") and s < NG - 1:
                        load_stack(b, s + 1)
                    if s == 0 and kind != "first":
                        load_max(b, 0)
                        load_res(b - 1)
                    if s == 1 and kind in ("first", "mid") and not cross:
                        store_h0(b + 1)
                    if s > 0 and kind != "tail":
                        if s == 3 and kind in ("first", "mid"):
                            store_parts(b + 1)
                            load_stack(b + 1, 0)
                        if s == 3 and kind != "first":
                            store_y(b - 1)
                        load_max(b, s)
                if kind == "tail":
                    store_y(b - 1)

            sp.dma_start(x_in[:, :, :], src[0].rearrange("(t p) d -> p t d", p=P)).then_inc(x_loaded, 16)
            for i, w in enumerate(cfg["w"]):
                sp.dma_start(w_raw[:, i], w.rearrange("(o p) i -> p o i", p=P)).then_inc(w_loaded, 16)
            if cross:
                sp.dma_start(gate[:, :], cfg["gate"].rearrange("(o n) -> o n", o=1).broadcast_to([P, 1])).then_inc(w_loaded, 16)
                with nc.allow_non_contiguous_dma(reason="a bias as columns, once"):
                    for i in range(2):
                        sp.dma_start(bias_col[:, i], cfg["bias"][i].rearrange("(g p) -> p g", p=P)).then_inc(w_loaded, 16)
                for i in range(2):
                    sp.dma_start(bias_row[:, i], cfg["bias"][2 + i].rearrange("(o n) -> o n", o=1).broadcast_to([P, D])
                                 ).then_inc(w_loaded, 16)
            else:
                with nc.allow_non_contiguous_dma(reason="a weight as columns, once"):
                    sp.dma_start(bias_col[:, 0], cfg["ln_w"].rearrange("(g p) -> p g", p=P)).then_inc(w_loaded, 16)
            if masked:
                sp.dma_start(mask_r[:, :], cfg["mask"]).then_inc(w_loaded, 16)
                sp.dma_start(mask_b[:, :], cfg["mask"][0:1, :].broadcast_to([P, S])).then_inc(c_loaded, 16)
            if cross:
                sp.dma_start(c_in[:, :, :], ctx_d[0].rearrange("(t p) d -> p t d", p=P)).then_inc(c_loaded, 16)
            if masked:
                sp.wait_ge(fill_chain, 3)
                sp.dma_start(fill[:, :, :], fill_p[:, :, :].bitcast(F32)).then_inc(fill_stored, 16)
                sp.wait_ge(fill_stored, 16)
            if not cross:
                store_h0(0)
            sp.wait_ge(rows_set, 4)
            store_parts(0)
            for g in range(NG):
                load_stack(0, g)
            unit(0, "first")
            unit(1, "mid")
            with sp.Fori(2, B - 1) as b:
                unit(b, "mid")
            unit(B - 1, "last")
            unit(B, "tail")
            sp.wait_ge(y_stored, 16 * B)

        @block.gpsimd
        def _(pool):
            def norm(b):
                pool.wait_ge(stats_made, b + 1)
                hold(pool, made["T"], 2 * b)
                factor = 1 if cross else 4
                for t in range(NT):
                    pool.tensor_scalar(x_norm[:, t, :], x_in[:, t, :], mean_var[:, t, 0:1],
                                       small[:, factor, t:t + 1], ALU.subtract, ALU.mult).then_inc(x_normed, 1)
                if not cross:
                    hold(pool, h0_stored, 16 * b)
                    for t in range(NT):
                        pool.tensor_scalar(h0[:, t, :], x_in[:, t, :], mean_var[:, t, 0:1],
                                           small[:, 1, t:t + 1], ALU.subtract, ALU.mult).then_inc(h0_made, 1)

            def low(b, g):
                for op, kind in ((0, "Q"), (1, "K")):
                    pool.wait_ge(taken[kind], 2 * b + g + 1)
                    after(pool, parts_stored, 64 * b)
                    pool.tensor_tensor(qk_parts[:, op, 1, g, :], qk_full[:, op, g, :],
                                       qk_parts[:, op, 0, g, :].bitcast(F32), ALU.subtract).then_inc(low_made, 1)

            def copy_v(b, g):
                pool.wait_ge(taken["V"], 2 * b + 2)
                hold(pool, pv_done, NT * (NG * (b - 1) + g + 1))
                pool.tensor_copy(v_aug[:, :, GH * g:GH * g + GH, 0:HD],
                                 v_new[:, :, 64 * g:64 * g + 64].rearrange("p t (h d) -> p t h d", d=HD)
                                 ).then_inc(v_copied, 1)

            def unit(b, kind):
                for s in range(NG):
                    if kind in ("mid", "last") and s < NG - 1:
                        copy_v(b, s + 1)
                    if kind in ("first", "mid"):
                        if s == 0:
                            norm(b + 1)
                        if s == 2:
                            low(b + 1, 0)
                            low(b + 1, 1)
                        if s == 3:
                            copy_v(b + 1, 0)

            pool.memset(ident[:, :], 0.0).then_inc(ident_made, 1)
            pool.wait_ge(ident_made, 1)
            pool.affine_select(out=ident[:, :], in_=ident[:, :], compare_op=ALU.not_equal, fill=1.0, base=0,
                               pattern=[[-1, P]], channel_multiplier=1).then_inc(ident_made, 1)
            norm(0)
            pool.memset(v_aug[:, :, :, :], 0.0).then_inc(v_set, 1)
            pool.wait_ge(v_set, 1)
            pool.memset(v_aug[:, :, :, HD:HD + 1], 1.0).then_inc(v_set, 1)
            low(0, 0)
            low(0, 1)
            for g in range(NG):
                copy_v(0, g)
            unit(0, "first")
            with pool.Fori(1, B - 1) as b:
                unit(b, "mid")
            unit(B - 1, "last")

        @block.tensor
        def _(pe):
            def piece(kind, off, bank, b, before):
                n = number(kind, off, b)
                if before is not None:
                    pk, poff = before
                    after(pe, taken[pk], number(pk, poff, b) + 1)
                out = ps_x[:, bank, :]
                c = off % 2
                if kind == "T":
                    pe.wait_ge(x_normed, NT * (b + 1) + NT)
                    for t in range(NT):
                        last = pe.transpose(out[:, t * P:t * P + P], x_norm[:, t, c * P:c * P + P], ident[:, :])
                elif kind == "C":
                    pe.wait_ge(c_loaded, (32 if masked else 16) * (b + 2))
                    for t in range(NT):
                        last = pe.transpose(out[:, t * P:t * P + P], c_in[:, t, c * P:c * P + P], ident[:, :])
                elif kind in ("Q", "K"):
                    from_t, w = (x_t, 0) if kind == "Q" else (c_t, 1)
                    pe.wait_ge(taken["C" if cross and kind == "K" else "T"], 2 * (b + 1) + 2)
                    for i in range(NC):
                        last = pe.matmul(out, w_t[:, w, i, c * P:c * P + P], from_t[:, i, :], start=(i == 0), stop=(i == NC - 1))
                elif kind == "V":
                    for t in (2 * c, 2 * c + 1):
                        for i in range(NC):
                            last = pe.matmul(out[:, (t % 2) * D:(t % 2) * D + D], c_t[:, i, t * P:t * P + P],
                                             w_t[:, 2, i, :], start=(i == 0), stop=(i == NC - 1))
                elif kind == "N":
                    pe.wait_ge(max_split, n + 1)
                    for t in range(NT):
                        last = pe.transpose(out[0:2 * GH, t * P:t * P + P],
                                            max_parts[:, t].rearrange("p r h -> p (r h)").bitcast(F32), ident[:, :])
                elif kind == "O":
                    pe.wait_ge(pv_taken, n + 1)
                    for t in range(NT):
                        last = pe.transpose(out[:, t * P:t * P + P], o_raw[:, t * P:t * P + P], ident[:, :])
                elif kind == "OT":
                    pe.wait_ge(taken["O"], NG * b)
                    for t in range(NT):
                        last = pe.transpose(out[:, t * P:t * P + P], o_tok[:, t, c * P:c * P + P], ident[:, :])
                elif kind == "Y":
                    pe.wait_ge(taken["OT"], 2 * (b - 1) + 2)
                    for t in (2 * c, 2 * c + 1):
                        for i in range(NC):
                            last = pe.matmul(out[:, (t % 2) * D:(t % 2) * D + D], o_t[:, i, t * P:t * P + P],
                                             w_t[:, 3, i, :], start=(i == 0), stop=(i == NC - 1))
                last.then_inc(made[kind], 1)

            def score_max(b, s, i):
                n = 16 * (NG * b + s) + i
                if i == 0:
                    pe.wait_ge(stack_loaded[s], (144 if masked else 128) * (b + 1))
                after(pe, maxed, n - 1)
                h, t = GH * s + i // NT, i % NT
                pe.matmul(ps_max[:, i % 2, :], q_stack[0:MAX_ROW, h, t * P:t * P + P], k_stack[0:MAX_ROW, h, :],
                          start=True, stop=True).then_inc(qk_scored, 1)

            def score_exp(b, s, kt, j):
                ge = (s - 2) % NG
                n = 16 * (NG * b + s - 2) + GH * kt + j
                if kt == 0 and j == 0:
                    pe.wait_ge(max_loaded[ge], 32 * (b + 1 if s >= 2 else b))
                after(pe, exped, n - 1)
                h = GH * ge + j
                pe.matmul(ps_exp[:, j % 2, :], k_stack[:, h, kt * P:kt * P + P], q_stack[:, h, :],
                          start=True, stop=True).then_inc(kq_scored, 1)

            def weigh(b, s, kt):
                g = s % NG
                n = NG * b + s
                pe.wait_ge(exped, 16 * n + GH * (kt + 1))
                if kt == 0:
                    pe.wait_ge(v_copied, n + 1)
                    after(pe, pv_taken, n - 1)
                for j in range(GH):
                    last = pe.matmul(ps_pv[VW * j:VW * j + VW, s % 2, :], v_aug[:, kt, GH * g + j, :],
                                     probs[:, kt, j, :], start=(kt == 0), stop=(kt == NT - 1),
                                     tile_position=(0, VW * j))
                last.then_inc(pv_done, 1)

            def unit(b, kind, before):
                before = dict(before)
                for s in range(NG):
                    for kt in range(NT):
                        for j in range(GH):
                            if kind != "tail":
                                score_max(b, s, GH * kt + j)
                            if (kind != "first" or s >= 2) and (kind != "tail" or s < 2):
                                score_exp(b, s, kt, j)
                        if kt == 0:
                            if (kind != "first" or s >= 3) and (kind != "tail" or s < 3):
                                weigh(b, s - 3, NT - 1)
                        elif (kind != "first" or s >= 2) and (kind != "tail" or s < 2):
                            weigh(b, s - 2, kt - 1)
                        for what, off, bank in pieces(kind, s, kt):
                            piece(what, off, bank, b, before[bank])
                            before[bank] = (what, off)
                return before

            pe.wait_ge(ident_made, 2)
            pe.wait_ge(w_loaded, 16 * W_DMAS)
            for i in range(8):
                m, c = i // NC, i % NC
                after(pe, w_taken, i - 1)
                for o in range(NC):
                    last = pe.transpose(ps_x[:, i % 2, o * P:o * P + P], w_raw[:, m, o, c * P:c * P + P], ident[:, :])
                last.then_inc(w_turned, 1)
            pe.wait_ge(w_taken, 8)
            before = {0: None, 1: None}
            for _, what, off, bank in table:
                if what in PREP:
                    piece(what, off, bank, -1, before[bank])
                    before[bank] = (what, off)
            before = {k: (what, off - 2) for k, (what, off) in before.items()}
            pe.wait_ge(rows_set, 4)
            pe.wait_ge(v_set, 2)
            unit(0, "first", before)
            steady = {table[-2][3]: ("N", -2), table[-1][3]: ("O", -4)}
            with pe.Fori(1, B - 1) as b:
                unit(b, "mid", steady)
            rest = unit(B - 1, "last", steady)
            unit(B, "tail", steady)

        @block.scalar
        def _(act):
            def take(kind, off, bank, b):
                n = number(kind, off, b)
                c = off % 2
                got = ps_x[:, bank, :]
                if kind == "T":
                    act.wait_ge(made[kind], n + 1)
                    if cross:
                        act.activation(x_t[:, c, :], got, ACT.Copy).then_inc(taken[kind], 1)
                    else:
                        act.activation(x_t[:, c, :], got, ACT.Identity, scale=bias_col[:, 0, c:c + 1]).then_inc(taken[kind], 1)
                elif kind == "C":
                    act.wait_ge(made[kind], n + 1)
                    act.activation(c_t[:, c, :], got, ACT.Copy).then_inc(taken[kind], 1)
                elif kind == "Q" or (kind == "K" and not K_BY_DVE):
                    op = 0 if kind == "Q" else 1
                    act.wait_ge(made[kind], n + 1)
                    after(act, low_made, 4 * (b + 1))
                    after(act, parts_stored, 64 * (b + 1))
                    bias = bias_col[:, op, c:c + 1] if cross else 0.0
                    act.activation(qk_full[:, op, c, :], got, ACT.Identity, bias=bias)
                    act.activation(qk_parts[:, op, 0, c, :], got, ACT.Identity, bias=bias).then_inc(taken[kind], 1)
                elif kind == "OT":
                    act.wait_ge(made[kind], n + 1)
                    act.activation(o_t[:, c, :], got, ACT.Copy).then_inc(taken[kind], 1)

            def exp(b, s, kt, j):
                n = 16 * (NG * b + s - 2) + GH * kt + j
                act.wait_ge(kq_scored, n + 1)
                if j == 0:
                    after(act, pv_done, NT * (NG * b + s - 3) + kt + 1)
                act.activation(probs[:, kt, j, :], ps_exp[:, j % 2, :], ACT.Exp, scale=SCALE).then_inc(exped, 1)

            def take_pv(b, s):
                n = NG * b + s
                act.wait_ge(pv_done, NT * n + NT)
                after(act, made["O"], n)
                act.activation(o_raw[:, :], ps_pv[:, s % 2, :], ACT.Copy).then_inc(pv_taken, 1)

            def unit(b, kind):
                for s in range(NG):
                    for kt in range(NT):
                        if (kind != "first" or s >= 2) and (kind != "tail" or s < 2):
                            for j in range(GH):
                                exp(b, s, kt, j)
                        if kt == 0 and (kind != "first" or s >= 3) and (kind != "tail" or s < 3):
                            take_pv(b, s - 3)
                        for what, off, bank in pieces(kind, s, kt):
                            take(what, off, bank, b)

            act.wait_ge(w_loaded, 16 * W_DMAS)
            if cross:
                act.activation(gate[:, :], gate[:, :], ACT.Tanh).then_inc(gate_made, 1)
            for i in range(8):
                act.wait_ge(w_turned, i + 1)
                act.activation(w_t[:, i // NC, i % NC, :], ps_x[:, i % 2, 0:D], ACT.Copy).then_inc(w_taken, 1)
            for _, what, off, bank in table:
                if what in PREP:
                    take(what, off, bank, -1)
            unit(0, "first")
            with act.Fori(1, B - 1) as b:
                unit(b, "mid")
            unit(B - 1, "last")
            unit(B, "tail")

        @block.vector
        def _(dve):
            def stats_of(b):
                dve.wait_ge(x_loaded, 16 * (b + 1))
                after(dve, x_normed, NT * b)
                count = [CHAIN * b]
                if not cross:
                    after(dve, h0_made, NT * b)

                def step(ins, wait=after):
                    count[0] = count[0] + 1
                    ins.then_inc(dve_chain, 1)
                    wait(dve, dve_chain, count[0])

                for t in range(NT):
                    last = dve.bn_stats(stats[:, t, :], x_in[:, t, :])
                step(last, hold)
                for t in range(NT):
                    last = dve.bn_aggr(mean_var[:, t, :], stats[:, t, :])
                step(last)
                step(dve.tensor_scalar(small[:, 0, :], mean_var[:, :, 1], EPS, None, ALU.add))
                emit_rsqrt(dve, step, small[:, 1, :], small[:, 0, :], small[:, 2, :])
                if not cross:
                    step(dve.tensor_tensor(small[:, 2, :], small[:, 1, :], small[:, 1, :], ALU.mult))
                    step(dve.tensor_tensor(small[:, 3, :], small[:, 2, :], mean_var[:, :, 1], ALU.mult))
                    step(dve.tensor_scalar(small[:, 0, :], small[:, 3, :], EPS, None, ALU.add))
                    emit_rsqrt(dve, step, small[:, 5, :], small[:, 0, :], small[:, 2, :])
                    step(dve.tensor_tensor(small[:, 4, :], small[:, 5, :], small[:, 1, :], ALU.mult))
                dve.sem_inc(stats_made, 1)

            def take(kind, off, bank, b):
                n = number(kind, off, b)
                c = off % 2
                got = ps_x[:, bank, :]
                if kind == "K" and K_BY_DVE:
                    dve.wait_ge(made[kind], n + 1)
                    dve.wait_ge(c_loaded, 32 * (b + 2))
                    after(dve, low_made, 4 * (b + 1))
                    after(dve, parts_stored, 64 * (b + 1))
                    for dst in (qk_full[:, 1, c, :], qk_parts[:, 1, 0, c, :]):
                        last = dve.scalar_tensor_tensor(dst, got, bias_col[:, 1, c:c + 1], mask_b[:, :], ALU.add, ALU.mult)
                    last.then_inc(taken[kind], 1)
                elif kind == "V":
                    dve.wait_ge(made[kind], n + 1)
                    after(dve, v_copied, NG * (b + 1))
                    dst = v_new[:, 2 * c:2 * c + 2, :]
                    both = got.rearrange("p (t d) -> p t d", d=D)
                    if cross:
                        dve.tensor_tensor(dst, both, bias_row[:, 0:1, :].broadcast_to([P, 2, D]), ALU.add).then_inc(taken[kind], 1)
                    else:
                        dve.tensor_copy(dst, both).then_inc(taken[kind], 1)
                elif kind == "N":
                    g = off % NG
                    dve.wait_ge(made[kind], n + 1)
                    after(dve, max_loaded[(g - 1) % NG], 32 * (b + 1 if off >= 1 else b))
                    dve.tensor_copy(max_rows[:, :], got[0:2 * GH, :]).then_inc(taken[kind], 1)
                elif kind == "O":
                    g = off % NG
                    dve.wait_ge(made[kind], n + 1)
                    if off == 0:
                        after(dve, made["OT"], 2 * b)
                    after(dve, taken[kind], n)
                    rows = got.rearrange("p (t h e) -> p t h e", t=NT, e=VW)
                    dve.reciprocal(rec[:, :, :], rows[:, :, :, HD]).then_inc(rec_made, 1)
                    dve.wait_ge(rec_made, n + 1)
                    dve.tensor_tensor(o_tok[:, :, 64 * g:64 * g + 64].rearrange("p t (h d) -> p t h d", d=HD),
                                      rows[:, :, :, 0:HD], rec[:, :, :].rearrange("p t (h o) -> p t h o", o=1).broadcast_to([P, NT, GH, HD]),
                                      ALU.mult).then_inc(taken[kind], 1)
                elif kind == "Y":
                    dve.wait_ge(made[kind], n + 1)
                    dve.wait_ge(res_loaded, 16 * b)
                    after(dve, y_stored, 16 * (b - 1))
                    tiles = slice(2 * c, 2 * c + 2)
                    both = got.rearrange("p (t d) -> p t d", d=D)
                    if cross:
                        after(dve, done_y, n)
                        dve.tensor_tensor(y_tmp[:, :, :], both, bias_row[:, 1:2, :].broadcast_to([P, 2, D]), ALU.add).then_inc(taken[kind], 1)
                        dve.wait_ge(taken[kind], n + 1)
                        dve.scalar_tensor_tensor(y_out[:, tiles, :], y_tmp[:, :, :], gate[:, 0:1], res[:, tiles, :],
                                                 ALU.mult, ALU.add).then_inc(done_y, 1)
                    else:
                        dve.tensor_tensor(y_out[:, tiles, :], both, res[:, tiles, :], ALU.add).then_inc(taken[kind], 1)
                        dve.wait_ge(taken[kind], n + 1)
                        dve.sem_inc(done_y, 1)

            def maxima(b, s, i):
                n = 16 * (NG * b + s) + i
                j, t = i // NT, i % NT
                dve.wait_ge(qk_scored, n + 1)
                dve.tensor_reduce(neg_max[:, t, j:j + 1], ps_max[:, i % 2, :], AX.X, ALU.max, negate=True).then_inc(maxed, 1)

            def split_max(b, s):
                n = NG * b + s
                dve.wait_ge(maxed, 16 * n + 16)
                after(dve, made["N"], n)
                dve.tensor_copy(max_parts[:, :, 0, :], neg_max[:, :, :]).then_inc(max_high, 1)
                dve.wait_ge(max_high, n + 1)
                dve.tensor_tensor(max_parts[:, :, 1, :], neg_max[:, :, :], max_parts[:, :, 0, :].bitcast(F32),
                                  ALU.subtract).then_inc(max_split, 1)

            def unit(b, kind):
                for s in range(NG):
                    for kt in range(NT):
                        if kind != "tail":
                            if kt == 0:
                                after(dve, max_split, NG * b + s)
                            for j in range(GH):
                                maxima(b, s, GH * kt + j)
                            if kt == NT - 1:
                                split_max(b, s)
                        if (s, kt) == (0, 1) and kind in ("first", "mid"):
                            stats_of(b + 1)
                        for what, off, bank in pieces(kind, s, kt):
                            take(what, off, bank, b)

            if masked:
                dve.wait_ge(w_loaded, 16 * W_DMAS)
                dve.tensor_scalar(fill_f[:, :], mask_r[:, :], -MASKED, MASKED, ALU.mult, ALU.add).then_inc(fill_chain, 1)
                dve.wait_ge(fill_chain, 1)
                dve.tensor_copy(fill_p[:, 0, :], fill_f[:, :]).then_inc(fill_chain, 1)
                dve.wait_ge(fill_chain, 2)
                dve.tensor_tensor(fill_p[:, 1, :], fill_f[:, :], fill_p[:, 0, :].bitcast(F32), ALU.subtract).then_inc(fill_chain, 1)
            stats_of(0)
            dve.memset(q_stack[64:P, :, :].bitcast(F32), 0.0).then_inc(rows_set, 1)
            dve.wait_ge(rows_set, 1)
            dve.memset(q_stack[ONE_ROW:ONE_ROW + 2, :, :].bitcast(F32), 1.0).then_inc(rows_set, 1)
            dve.memset(k_stack[64:P, :, :].bitcast(F32), 1.0).then_inc(rows_set, 1)
            dve.wait_ge(rows_set, 3)
            dve.memset(k_stack[ONE_ROW:ONE_ROW + 2, :, :].bitcast(F32), 0.0).then_inc(rows_set, 1)
            dve.wait_ge(w_loaded, 16 * W_DMAS)
            if cross:
                dve.wait_ge(gate_made, 1)
            for _, what, off, bank in table:
                if what in PREP:
                    take(what, off, bank, -1)
            unit(0, "first")
            unit(1, "mid")
            with dve.Fori(2, B - 1) as b:
                unit(b, "mid")
            unit(B - 1, "last")
            unit(B, "tail")

E0, FF = 8, 512
E1, RANK = 8, 64
NF = FF // P
NB = B
PASSES = ((0, 0), (0, 1), (1, 0))


class Chain:

    def __init__(self, dve, sem, start):
        self.dve, self.sem, self.at = dve, sem, start

    def __call__(self, ins, wait=after):
        self.at = self.at + 1
        ins.then_inc(self.sem, 1)
        wait(self.dve, self.sem, self.at)


def emit_top2(dve, step, tiles, made_gap, exp_done, n, out):
    logits, best, where, place, iota, g = (tiles[k] for k in ("logits", "best", "where", "place", "iota", "g"))
    for t in range(NT):
        last = dve.max(best[:, t, :], logits[:, t, :])
    step(last, hold)
    for t in range(NT):
        last = dve.max_index(where[:, t, :], best[:, t, :], logits[:, t, :])
    step(last)
    dve.tensor_tensor(g[:, 0, :], best[:, :, 1], best[:, :, 0], ALU.subtract).then_inc(made_gap, 1)
    step(dve.tensor_copy(place[:, :, :], where[:, :, 0:2]))
    one_hot = tiles["one_hot"]
    for k in range(2):
        last = dve.tensor_tensor(one_hot[:, k], iota[:, :, :], place[:, :, k:k + 1].broadcast_to([P, NT, 8]), ALU.is_equal)
    step(last)
    dve.wait_ge(exp_done, n + 1)
    step(dve.tensor_scalar(g[:, 2, :], g[:, 1, :], 1.0, None, ALU.add))
    step(dve.reciprocal(g[:, 3, :], g[:, 2, :]))
    step(dve.tensor_tensor(g[:, 4, :], g[:, 1, :], g[:, 3, :], ALU.mult))
    for k in range(2):
        last = dve.tensor_tensor(one_hot[:, k], one_hot[:, k],
                                 g[:, 3 + k, :].rearrange("p (t o) -> p t o", o=1).broadcast_to([P, NT, 8]), ALU.mult)
    step(last)
    step(dve.tensor_tensor(out, one_hot[:, 0], one_hot[:, 1], ALU.add))


TOP2_STEPS = 9


def top2_tiles(sb):
    return {
        "logits": sb("logits", [P, NT, 8]), "best": sb("best", [P, NT, 8]), "where": sb("where", [P, NT, 8], U32),
        "place": sb("place", [P, NT, 2]), "iota": sb("iota", [P, NT, 8]), "one_hot": sb("one_hot", [P, 2, NT, 8]),
        "g": sb("g", [P, 5, NT]),
    }


def emit_ident(pool, ident, made):
    pool.memset(ident[:, :], 0.0).then_inc(made, 1)
    pool.wait_ge(made, 1)
    pool.affine_select(out=ident[:, :], in_=ident[:, :], compare_op=ALU.not_equal, fill=1.0, base=0,
                       pattern=[[-1, P]], channel_multiplier=1).then_inc(made, 1)


def by_token(dram, b):
    return dram[b].rearrange("(t p) d -> p t d", p=P)


def build_swiglu_moe(nc, tag, cfg):
    h_d, x_d, out_d = cfg["h"], cfg["x"], cfg["out"]
    with ExitStack() as stack:
        def sb(name, shape, dt=F32):
            return stack.enter_context(nc.sbuf_tensor(f"{tag}_{name}", shape, dt))

        def ps(name, shape):
            return stack.enter_context(nc.psum_tensor(f"{tag}_{name}", shape, F32))

        def sem(name):
            return stack.enter_context(nc.semaphore(f"{tag}_{name}"))

        ident = sb("ident", [P, P])
        ln_col = sb("ln_col", [P, NC])
        gate = sb("gate", [P, 1])
        gw_raw = sb("gw_raw", [E0, D])
        gw_t = sb("gw_t", [P, NC, E0])
        h_in = sb("h_in", [P, NT, D])
        n_tok = sb("n_tok", [P, NT, D])
        stats, mean_var, small = sb("stats", [P, NT, 6]), sb("mean_var", [P, NT, 2]), sb("small", [P, 4, NT])
        n_full = sb("n_full", [P, NC, S])
        n_part = [sb(f"n_part{i}", [P, NC, B * S], F32R) for i in range(2)]
        tiles = top2_tiles(sb)
        gates = sb("gates", [P, NB * NT, E0])
        acc = sb("acc", [P, NB * NT, D])
        raw13 = sb("raw13", [P, 2, NF, D])
        raw2 = sb("raw2", [P, NC, FF])
        w13 = [[sb(f"w13_{q}{part}", [P, 2, NC, FF], F32R) for part in range(2)] for q in range(2)]
        w2 = [[sb(f"w2_{q}{part}", [P, NF, D], F32R) for part in range(2)] for q in range(2)]
        silu = n_full
        hid = sb("hid", [P, 2, S])
        hid_part = [[sb(f"hid_{q}{part}", [P, NF, S], F32R) for part in range(2)] for q in range(2)]

        ps_g = ps("ps_g", [P, 2, S])
        ps_u = ps("ps_u", [P, 2, S])
        ps_y = ps("ps_y", [P, 2, S])
        ps_w = ps("ps_w", [P, 2, S])

        ident_made, const_loaded, gate_made, gw_made, gw_taken, iota_made = (sem(n) for n in (
            "ident_made", "const_loaded", "gate_made", "gw_made", "gw_taken", "iota_made"))
        h_loaded, acc_loaded, chain_sem, stats_made, normed = (sem(n) for n in (
            "h_loaded", "acc_loaded", "chain", "stats_made", "normed"))
        turned, t_taken, low_made, logit_made, logit_taken, gap_made, exp_made, gates_made = (sem(n) for n in (
            "turned", "t_taken", "low_made", "logit_made", "logit_taken", "gap_made", "exp_made", "gates_made"))
        raw_loaded, w_turned, w_high, w_low = (sem(n) for n in ("raw_loaded", "w_turned", "w_high", "w_low"))
        g_made, u_made, silu_made, hid_made, hid_high, hid_low = (sem(n) for n in (
            "g_made", "u_made", "silu_made", "hid_made", "hid_high", "hid_low"))
        y_made, y_taken = sem("y_made"), sem("y_taken")
        x_loaded = [sem(f"x_loaded{i}") for i in range(2)]
        out_made, out_stored = sem("out_made"), [sem(f"out_stored{i}") for i in range(2)]

        NEWTON = 11
        CH = 4 + NEWTON
        block = stack.enter_context(nc.Block())

        @block.sync
        def _(sp):
            def load_raw(e):
                after(sp, w_turned, 6 * e)
                sp.dma_start(raw13[:, 0], cfg["w1"][e].rearrange("(o p) i -> p o i", p=P)).then_inc(raw_loaded, 16)
                sp.dma_start(raw13[:, 1], cfg["w3"][e].rearrange("(o p) i -> p o i", p=P)).then_inc(raw_loaded, 16)
                sp.dma_start(raw2[:, :, :], cfg["w2"][e].rearrange("(o p) i -> p o i", p=P)).then_inc(raw_loaded, 16)

            sp.dma_start(h_in[:, :, :], by_token(h_d, 0)).then_inc(h_loaded, 16)
            with nc.allow_non_contiguous_dma(reason="a weight as columns, once"):
                sp.dma_start(ln_col[:, :], cfg["ln_w"].rearrange("(g p) -> p g", p=P)).then_inc(const_loaded, 16)
            sp.dma_start(gate[:, :], cfg["gate"].rearrange("(o n) -> o n", o=1).broadcast_to([P, 1])).then_inc(const_loaded, 16)
            sp.dma_start(gw_raw[:, :], cfg["gate_w"]).then_inc(const_loaded, 16)
            load_raw(0)
            sp.dma_start(acc[:, :, :], h_d[:, :, :].rearrange("b (t p) d -> p (b t) d", p=P)).then_inc(acc_loaded, 16)
            with sp.Fori(1, NB) as b:
                sp.wait_ge(normed, NT * b)
                sp.dma_start(h_in[:, :, :], by_token(h_d, b)).then_inc(h_loaded, 16)
            with sp.Fori(1, E0) as e:
                load_raw(e)
            for i, dst in enumerate((h_in, n_tok)):
                sp.wait_ge(turned, 2 * NB)
                sp.dma_start(dst[:, :, :], by_token(x_d, i)).then_inc(x_loaded[i], 16)
            for b in range(NB):
                sp.wait_ge(out_made, b + 1)
                sp.dma_start(by_token(out_d, b), acc[:, NT * b:NT * b + NT, :]).then_inc(out_stored[b % 2], 16)
                if b + 2 < NB:
                    sp.dma_start((h_in, n_tok)[b % 2][:, :, :], by_token(x_d, b + 2)).then_inc(x_loaded[b % 2], 16)
            for i in range(2):
                sp.wait_ge(out_stored[i], 16 * NB // 2)

        @block.gpsimd
        def _(pool):
            emit_ident(pool, ident, ident_made)
            for e in range(E0):
                last = pool.memset(tiles["iota"][:, :, e:e + 1], float(e))
                last.then_inc(iota_made, 1)

            def norm_and_low(b):
                pool.wait_ge(stats_made, b + 1)
                hold(pool, turned, 2 * b)
                for t in range(NT):
                    pool.tensor_scalar(n_tok[:, t, :], h_in[:, t, :], small[:, 1, t:t + 1], None, ALU.mult).then_inc(normed, 1)
                for c in range(NC):
                    pool.wait_ge(t_taken, 2 * b + c + 1)
                    at = bass.ds(b * S, S)
                    pool.tensor_tensor(n_part[1][:, c, at], n_full[:, c, :], n_part[0][:, c, at].bitcast(F32),
                                       ALU.subtract).then_inc(low_made, 1)

            norm_and_low(0)
            with pool.Fori(1, NB) as b:
                norm_and_low(b)

            with pool.Fori(0, E0 // 2) as pair:
                for q in range(2):
                    for b in range(NB):
                        for f in range(NF):
                            n = (2 * pair + q) * NB * NF + b * NF + f
                            pool.wait_ge(hid_high, n + 1)
                            pool.tensor_tensor(hid_part[b % 2][1][:, f, :], hid[:, f % 2, :],
                                               hid_part[b % 2][0][:, f, :].bitcast(F32), ALU.subtract).then_inc(hid_low, 1)

        def weight_piece(i):
            if i < 4:
                m, c = i // 2, i % 2
                return [raw13[:, m, o, c * P:c * P + P] for o in range(NF)], lambda w: w13[w[0]][w[1]][:, m, c, :]
            f = 2 * (i - 4)
            return ([raw2[:, o, (f + k) * P:(f + k) * P + P] for k in range(2) for o in range(NC)],
                    lambda w: w2[w[0]][w[1]][:, f:f + 2, :].rearrange("p f d -> p (f d)"))

        @block.tensor
        def _(pe):
            def turn_weights(e, i):
                if i == 0:
                    pe.wait_ge(raw_loaded, 48 * (e + 1))
                after(pe, w_low, 6 * e + i - 1)
                for k, blk in enumerate(weight_piece(i)[0]):
                    last = pe.transpose(ps_w[:, i % 2, k * P:k * P + P], blk, ident[:, :])
                last.then_inc(w_turned, 1)

            pe.wait_ge(ident_made, 2)
            pe.wait_ge(const_loaded, 48)
            for c in range(NC):
                last = pe.transpose(ps_y[:, 0, c * E0:c * E0 + E0], gw_raw[:, c * P:c * P + P], ident[0:E0, 0:E0])
            last.then_inc(gw_made, 1)
            for i in range(6):
                turn_weights(0, i)
            pe.wait_ge(gw_taken, 1)
            def turn_and_score(b):
                pe.wait_ge(normed, NT * b + NT)
                for c in range(NC):
                    after(pe, t_taken, 2 * b)
                    for t in range(NT):
                        last = pe.transpose(ps_g[:, c, t * P:t * P + P], n_tok[:, t, c * P:c * P + P], ident[:, :])
                    last.then_inc(turned, 1)
                pe.wait_ge(t_taken, 2 * b + 2)
                after(pe, logit_taken, b)
                for t in range(NT):
                    for c in range(NC):
                        last = pe.matmul(ps_u[:, 0, t * E0:t * E0 + E0], n_full[:, c, t * P:t * P + P], gw_t[:, c, :],
                                         start=(c == 0), stop=(c == NC - 1))
                last.then_inc(logit_made, 1)

            turn_and_score(0)
            with pe.Fori(1, NB) as b:
                turn_and_score(b)

            def project(which, dst, free, made_sem, n, q, b, f):
                after(pe, free, n - 1)
                k = 0
                for c in range(NC):
                    for wp, ap in PASSES:
                        last = pe.matmul(dst[:, f % 2, :], w13[q][wp][:, which, c, f * P:f * P + P],
                                         n_part[ap][:, c, b * S:b * S + S], start=(k == 0), stop=(k == 5))
                        k += 1
                last.then_inc(made_sem, 1)

            def down(q, b, t, n):
                if t == 0:
                    pe.wait_ge(hid_low, NF * n + NF)
                after(pe, y_taken, NT * n + t - 1)
                k = 0
                for f in range(NF):
                    for wp, ap in PASSES:
                        last = pe.matmul(ps_y[:, t % 2, 0:D],
                                         hid_part[b % 2][ap][:, f, t * P:t * P + P], w2[q][wp][:, f, :],
                                         start=(k == 0), stop=(k == 3 * NF - 1))
                        k += 1
                last.then_inc(y_made, 1)

            def expert(e, q, first, last_one):
                pe.wait_ge(w_low, 6 * e + 6)
                for b in range(NB):
                    for f in range(NF):
                        n = (e * NB + b) * NF + f
                        project(0, ps_g, silu_made, g_made, n, q, b, f)
                        project(1, ps_u, hid_high, u_made, n, q, b, f)
                        if b > 0:
                            down(q, b - 1, f, e * NB + b - 1)
                        elif not first:
                            down(1 - q, NB - 1, f, e * NB - 1)
                    if b >= 1 and b < 7 and not last_one:
                        turn_weights(e + 1, b - 1)

            pe.wait_ge(low_made, 2 * NB)
            pe.wait_ge(logit_taken, NB)
            expert(0, 0, True, False)
            with pe.Fori(0, E0 // 2 - 1) as pair:
                expert(2 * pair + 1, 1, False, False)
                expert(2 * pair + 2, 0, False, False)
            expert(E0 - 1, 1, False, True)
            for t in range(NT):
                down(1, NB - 1, t, E0 * NB - 1)

        @block.scalar
        def _(act):
            def take_weights(e, q, i):
                act.wait_ge(w_turned, 6 * e + i + 1)
                act.activation(weight_piece(i)[1]((q, 0)), ps_w[:, i % 2, :], ACT.Copy).then_inc(w_high, 1)

            act.wait_ge(const_loaded, 48)
            act.activation(gate[:, :], gate[:, :], ACT.Tanh).then_inc(gate_made, 1)
            for i in range(6):
                take_weights(0, 0, i)
            def take_tokens(b):
                after(act, low_made, 2 * b)
                after(act, logit_made, b)
                for c in range(NC):
                    act.wait_ge(turned, 2 * b + c + 1)
                    act.activation(n_full[:, c, :], ps_g[:, c, :], ACT.Identity, scale=ln_col[:, c:c + 1])
                    act.activation(n_part[0][:, c, bass.ds(b * S, S)], ps_g[:, c, :], ACT.Identity,
                                   scale=ln_col[:, c:c + 1]).then_inc(t_taken, 1)
                act.wait_ge(gap_made, b + 1)
                act.activation(tiles["g"][:, 1, :], tiles["g"][:, 0, :], ACT.Exp).then_inc(exp_made, 1)

            take_tokens(0)
            with act.Fori(1, NB) as b:
                take_tokens(b)

            def expert(e, q, last_one):
                for b in range(NB):
                    for f in range(NF):
                        n = (e * NB + b) * NF + f
                        act.wait_ge(g_made, n + 1)
                        after(act, hid_high, n - 1)
                        act.activation(silu[:, f % 2, :], ps_g[:, f % 2, :], ACT.Silu).then_inc(silu_made, 1)
                    if b >= 1 and b < 7 and not last_one:
                        take_weights(e + 1, 1 - q, b - 1)

            act.wait_ge(low_made, 2 * NB)
            act.wait_ge(logit_made, NB)
            expert(0, 0, False)
            with act.Fori(0, E0 // 2 - 1) as pair:
                expert(2 * pair + 1, 1, False)
                expert(2 * pair + 2, 0, False)
            expert(E0 - 1, 1, True)

        @block.vector
        def _(dve):
            def low_weights(e, q, i):
                dve.wait_ge(w_high, 6 * e + i + 1)
                to = weight_piece(i)[1]
                dve.tensor_tensor(to((q, 1)), ps_w[:, i % 2, :], to((q, 0)).bitcast(F32), ALU.subtract).then_inc(w_low, 1)

            dve.wait_ge(gw_made, 1)
            dve.tensor_copy(gw_t[:, :, :].rearrange("p c e -> p (c e)"), ps_y[:, 0, 0:NC * E0]).then_inc(gw_taken, 1)
            for i in range(6):
                low_weights(0, 0, i)
            dve.wait_ge(iota_made, E0)
            def gating(b):
                step = Chain(dve, chain_sem, (CH + TOP2_STEPS) * b)
                dve.wait_ge(h_loaded, 16 * (b + 1))
                after(dve, normed, NT * b)
                for t in range(NT):
                    last = dve.bn_stats(stats[:, t, :], h_in[:, t, :])
                step(last, hold)
                for t in range(NT):
                    last = dve.bn_aggr(mean_var[:, t, :], stats[:, t, :])
                step(last)
                step(dve.tensor_tensor(small[:, 2, :], mean_var[:, :, 0], mean_var[:, :, 0], ALU.mult))
                step(dve.scalar_tensor_tensor(small[:, 0, :], small[:, 2, :], EPS, mean_var[:, :, 1], ALU.add, ALU.add))
                emit_rsqrt(dve, step, small[:, 1, :], small[:, 0, :], small[:, 2, :])
                dve.sem_inc(stats_made, 1)
                dve.wait_ge(logit_made, b + 1)
                dve.tensor_copy(tiles["logits"][:, :, :].rearrange("p t e -> p (t e)"), ps_u[:, 0, 0:NT * E0]).then_inc(logit_taken, 1)
                hold(dve, logit_taken, b + 1)
                emit_top2(dve, step, tiles, gap_made, exp_made, b, gates[:, bass.ds(NT * b, NT), :])

            gating(0)
            with dve.Fori(1, NB) as b:
                gating(b)

            def add_tile(n, b, t, e):
                dve.wait_ge(y_made, NT * n + t + 1)
                tile = NT * b + t
                dve.scalar_tensor_tensor(acc[:, tile, :], ps_y[:, t % 2, 0:D],
                                         gates[:, tile, bass.ds(e, 1)], acc[:, tile, :], ALU.mult, ALU.add).then_inc(y_taken, 1)

            def expert(e, q, first, last_one):
                for b in range(NB):
                    for f in range(NF):
                        n = (e * NB + b) * NF + f
                        dve.wait_ge(u_made, n + 1)
                        dve.wait_ge(silu_made, n + 1)
                        after(dve, hid_low, n - 1)
                        if f == 0:
                            after(dve, y_made, NT * (e * NB + b - 1))
                        dve.tensor_tensor(hid[:, f % 2, :], silu[:, f % 2, :], ps_u[:, f % 2, :], ALU.mult)
                        dve.tensor_tensor(hid_part[b % 2][0][:, f, :], silu[:, f % 2, :], ps_u[:, f % 2, :],
                                          ALU.mult).then_inc(hid_high, 1)
                        if b > 0:
                            add_tile(e * NB + b - 1, b - 1, f, e)
                        elif not first:
                            add_tile(e * NB - 1, NB - 1, f, e - 1)
                    if b >= 1 and b < 7 and not last_one:
                        low_weights(e + 1, 1 - q, b - 1)

            dve.wait_ge(acc_loaded, 16)
            expert(0, 0, True, False)
            with dve.Fori(0, E0 // 2 - 1) as pair:
                expert(2 * pair + 1, 1, False, False)
                expert(2 * pair + 2, 0, False, False)
            expert(E0 - 1, 1, False, True)
            for t in range(NT):
                add_tile(E0 * NB - 1, NB - 1, t, E0 - 1)
            dve.wait_ge(y_taken, E0 * NB * NT)
            dve.wait_ge(gate_made, 1)
            for b in range(NB):
                dve.wait_ge(x_loaded[b % 2], 16 * (b // 2 + 1))
                here = acc[:, NT * b:NT * b + NT, :]
                dve.scalar_tensor_tensor(here, here, gate[:, 0:1], (h_in, n_tok)[b % 2][:, :, :], ALU.mult, ALU.add).then_inc(out_made, 1)


def build_lora_moe(nc, tag, cfg):
    x_d, out_d = cfg["x"], cfg["out"]
    NQ = E1 * RANK // P
    with ExitStack() as stack:
        def sb(name, shape, dt=F32):
            return stack.enter_context(nc.sbuf_tensor(f"{tag}_{name}", shape, dt))

        def ps(name, shape):
            return stack.enter_context(nc.psum_tensor(f"{tag}_{name}", shape, F32))

        def sem(name):
            return stack.enter_context(nc.semaphore(f"{tag}_{name}"))

        ident = sb("ident", [P, P])
        gate = sb("gate", [P, 1])
        gate2 = sb("gate2", [P, 1])
        bg = sb("bg", [P, 1, E1])
        wg_raw = sb("wg_raw", [E1, D])
        wg_t = sb("wg_t", [P, NC, E1])
        w1_raw = sb("w1_raw", [P, NQ, D])
        w1_t = sb("w1_t", [P, NC, NQ * P])
        w2_raw = sb("w2_raw", [P, NC, E1, RANK])
        w2_t = sb("w2_t", [P, NQ, D])
        spread = sb("spread", [E1, NQ * P])
        x_in = sb("x_in", [P, NT, D])
        res = sb("res", [P, NT, D])
        stats, mean_var, small = sb("stats", [P, NT, 6]), sb("mean_var", [P, NT, 2]), sb("small", [P, 4, NT])
        n_tok = sb("n_tok", [P, NT, D])
        n_t = sb("n_t", [P, NC, S])
        tiles = top2_tiles(sb)
        gates = sb("gates", [P, NT, E1])
        gates_t = sb("gates_t", [E1, S])
        hid = sb("hid", [P, NQ, S])
        hid_g = sb("hid_g", [P, NQ, S])
        y_out = sb("y_out", [P, NT, D])

        ps_t = ps("ps_t", [P, 2, S])
        ps_h = ps("ps_h", [P, 2, S])
        ps_e = ps("ps_e", [P, 2, S])
        ps_y = ps("ps_y", [P, 2, S])

        ident_made, const_loaded, gate_made, w_made, w_taken, iota_made, spread_made = (sem(n) for n in (
            "ident_made", "const_loaded", "gate_made", "w_made", "w_taken", "iota_made", "spread_made"))
        x_loaded, res_loaded, chain_sem, stats_made, normed, out_stored = (sem(n) for n in (
            "x_loaded", "res_loaded", "chain", "stats_made", "normed", "out_stored"))
        turned, t_taken, logit_made, logit_taken, gap_made, exp_made, gates_made, gt_made, gt_taken = (sem(n) for n in (
            "turned", "t_taken", "logit_made", "logit_taken", "gap_made", "exp_made", "gates_made", "gt_made", "gt_taken"))
        h_made, gelu_made, e_made, gated, y_made, y_taken = (sem(n) for n in (
            "h_made", "gelu_made", "e_made", "gated", "y_made", "y_taken"))
        NEWTON = 11
        CH = 3 + NEWTON
        TOP = TOP2_STEPS
        N_CONST = 6
        block = stack.enter_context(nc.Block())

        @block.sync
        def _(sp):
            sp.dma_start(x_in[:, :, :], by_token(x_d, 0)).then_inc(x_loaded, 16)
            sp.dma_start(gate[:, :], cfg["gate"].rearrange("(o n) -> o n", o=1).broadcast_to([P, 1])).then_inc(const_loaded, 16)
            sp.dma_start(bg[:, 0, :], cfg["bg"].rearrange("(o n) -> o n", o=1).broadcast_to([P, E1])).then_inc(const_loaded, 16)
            sp.dma_start(wg_raw[:, :], cfg["wg"]).then_inc(const_loaded, 16)
            sp.dma_start(w1_raw[:, :, :], cfg["w1"].rearrange("e r d -> (e r) d").rearrange("(q p) d -> p q d", p=P)
                         ).then_inc(const_loaded, 16)
            for c in range(NC):
                sp.dma_start(w2_raw[:, c], cfg["w2"][:, c * P:c * P + P, :].rearrange("e p r -> p e r")).then_inc(const_loaded, 16)

            def fetch(b):
                sp.wait_ge(normed, NT * b)
                sp.dma_start(x_in[:, :, :], by_token(x_d, b)).then_inc(x_loaded, 16)

            def unit(b, more):
                if more:
                    fetch(b + 1)
                after(sp, y_taken, 2 * b)
                sp.dma_start(res[:, :, :], by_token(x_d, b)).then_inc(res_loaded, 16)
                sp.wait_ge(y_taken, 2 * b + 2)
                sp.dma_start(by_token(out_d, b), y_out[:, :, :]).then_inc(out_stored, 16)

            unit(0, True)
            with sp.Fori(1, B - 1) as b:
                unit(b, True)
            unit(B - 1, False)
            sp.wait_ge(out_stored, 16 * B)

        @block.gpsimd
        def _(pool):
            emit_ident(pool, ident, ident_made)
            for e in range(E1):
                pool.memset(tiles["iota"][:, :, e:e + 1], float(e)).then_inc(iota_made, 1)
            pool.memset(spread[:, :], 1.0).then_inc(spread_made, 1)
            pool.wait_ge(spread_made, 1)
            pool.affine_select(out=spread[:, :], in_=spread[:, :], compare_op=ALU.is_ge, fill=0.0, base=0,
                               pattern=[[1, NQ * P]], channel_multiplier=-RANK).then_inc(spread_made, 1)
            pool.wait_ge(spread_made, 2)
            pool.affine_select(out=spread[:, :], in_=spread[:, :], compare_op=ALU.is_ge, fill=0.0, base=RANK - 1,
                               pattern=[[-1, NQ * P]], channel_multiplier=RANK).then_inc(spread_made, 1)

            def norm(b):
                pool.wait_ge(stats_made, b + 1)
                hold(pool, turned, 2 * b)
                for t in range(NT):
                    pool.tensor_scalar(n_tok[:, t, :], x_in[:, t, :], mean_var[:, t, 0:1], small[:, 1, t:t + 1],
                                       ALU.subtract, ALU.mult).then_inc(normed, 1)
            norm(0)
            with pool.Fori(0, B - 1) as b:
                norm(b + 1)

        @block.tensor
        def _(pe):
            pe.wait_ge(ident_made, 2)
            pe.wait_ge(const_loaded, 16 * N_CONST)
            for c in range(NC):
                for q in range(NQ):
                    last = pe.transpose(ps_h[:, c, q * P:q * P + P], w1_raw[:, q, c * P:c * P + P], ident[:, :])
                last.then_inc(w_made, 1)
            for q in range(NQ):
                for c in range(NC):
                    last = pe.transpose(ps_e[:, q // 2, (q % 2) * D + c * P:(q % 2) * D + c * P + P],
                                        w2_raw[:, c, 2 * q:2 * q + 2, :].rearrange("p e r -> p (e r)"), ident[:, :])
                if q % 2:
                    last.then_inc(w_made, 1)
            for c in range(NC):
                last = pe.transpose(ps_y[:, 0, c * E1:c * E1 + E1], wg_raw[:, c * P:c * P + P], ident[0:E1, 0:E1])
            last.then_inc(w_made, 1)
            pe.wait_ge(w_taken, 5)
            pe.wait_ge(spread_made, 3)

            def turn(b):
                pe.wait_ge(normed, NT * b + NT)
                for c in range(NC):
                    after(pe, t_taken, 2 * b)
                    for t in range(NT):
                        last = pe.transpose(ps_t[:, c, t * P:t * P + P], n_tok[:, t, c * P:c * P + P], ident[:, :])
                    last.then_inc(turned, 1)

            def logits(b):
                pe.wait_ge(t_taken, 2 * b + 2)
                after(pe, gt_taken, b)
                for t in range(NT):
                    for c in range(NC):
                        last = pe.matmul(ps_t[:, 0, t * E1:t * E1 + E1], n_t[:, c, t * P:t * P + P], wg_t[:, c, :],
                                         start=(c == 0), stop=(c == NC - 1))
                last.then_inc(logit_made, 1)

            def turn_gates(b):
                pe.wait_ge(gates_made, b + 1)
                for t in range(NT):
                    last = pe.transpose(ps_t[0:E1, 1, t * P:t * P + P], gates[:, t, :], ident[:, :])
                last.then_inc(gt_made, 1)

            def experts_in(b):
                for q in range(NQ):
                    after(pe, gelu_made, NQ * b + q - 1)
                    for c in range(NC):
                        last = pe.matmul(ps_h[:, q % 2, :], w1_t[:, c, q * P:q * P + P], n_t[:, c, :],
                                         start=(c == 0), stop=(c == NC - 1))
                    last.then_inc(h_made, 1)
                    if q == 0:
                        pe.wait_ge(gt_taken, b + 1)
                    after(pe, gated, NQ * b + q - 1)
                    pe.matmul(ps_e[:, q % 2, :], spread[:, q * P:q * P + P], gates_t[:, :],
                              start=True, stop=True).then_inc(e_made, 1)

            def experts_out(b):
                pe.wait_ge(gated, NQ * b + NQ)
                for t in range(NT):
                    if t % 2 == 0:
                        after(pe, y_taken, 2 * b + t // 2 - 1)
                    for q in range(NQ):
                        last = pe.matmul(ps_y[:, t // 2, (t % 2) * D:(t % 2) * D + D], hid_g[:, q, t * P:t * P + P],
                                         w2_t[:, q, :], start=(q == 0), stop=(q == NQ - 1))
                    if t % 2:
                        last.then_inc(y_made, 1)

            def unit(b, more):
                experts_in(b)
                if more:
                    turn(b + 1)
                    logits(b + 1)
                experts_out(b)
                if more:
                    turn_gates(b + 1)

            turn(0)
            logits(0)
            turn_gates(0)
            unit(0, True)
            with pe.Fori(1, B - 1) as b:
                unit(b, True)
            unit(B - 1, False)

        @block.scalar
        def _(act):
            act.wait_ge(const_loaded, 16 * N_CONST)
            act.activation(gate[:, :], gate[:, :], ACT.Tanh).then_inc(gate_made, 1)

            def take(b):
                for c in range(NC):
                    act.wait_ge(turned, 2 * b + c + 1)
                    if c == 0:
                        after(act, h_made, NQ * b)
                    act.activation(n_t[:, c, :], ps_t[:, c, :], ACT.Copy).then_inc(t_taken, 1)
                act.wait_ge(gap_made, b + 1)
                act.activation(tiles["g"][:, 1, :], tiles["g"][:, 0, :], ACT.Exp).then_inc(exp_made, 1)

            def gelus(b):
                for q in range(NQ):
                    act.wait_ge(h_made, NQ * b + q + 1)
                    after(act, gated, NQ * (b - 1) + q + 1)
                    act.activation(hid[:, q, :], ps_h[:, q % 2, :], ACT.Gelu).then_inc(gelu_made, 1)

            def unit(b, more):
                gelus(b)
                if more:
                    take(b + 1)

            take(0)
            unit(0, True)
            with act.Fori(1, B - 1) as b:
                unit(b, True)
            unit(B - 1, False)

        @block.vector
        def _(dve):
            for c in range(NC):
                dve.wait_ge(w_made, c + 1)
                dve.tensor_copy(w1_t[:, c, :], ps_h[:, c, :]).then_inc(w_taken, 1)
            for k in range(2):
                dve.wait_ge(w_made, k + 3)
                dve.tensor_copy(w2_t[:, 2 * k:2 * k + 2, :].rearrange("p q d -> p (q d)"), ps_e[:, k, :]).then_inc(w_taken, 1)
            dve.wait_ge(w_made, 5)
            dve.tensor_copy(wg_t[:, :, :].rearrange("p c e -> p (c e)"), ps_y[:, 0, 0:NC * E1]).then_inc(w_taken, 1)
            dve.wait_ge(gate_made, 1)
            dve.tensor_scalar(gate2[:, :], gate[:, :], 2.0, None, ALU.mult).then_inc(w_taken, 1)
            dve.wait_ge(w_taken, 6)
            dve.wait_ge(iota_made, E1)

            def stats_of(b):
                step = Chain(dve, chain_sem, (CH + TOP) * b)
                dve.wait_ge(x_loaded, 16 * (b + 1))
                after(dve, normed, NT * b)
                for t in range(NT):
                    last = dve.bn_stats(stats[:, t, :], x_in[:, t, :])
                step(last, hold)
                for t in range(NT):
                    last = dve.bn_aggr(mean_var[:, t, :], stats[:, t, :])
                step(last)
                step(dve.tensor_scalar(small[:, 0, :], mean_var[:, :, 1], EPS, None, ALU.add))
                emit_rsqrt(dve, step, small[:, 1, :], small[:, 0, :], small[:, 2, :])
                dve.sem_inc(stats_made, 1)

            def gating(b):
                step = Chain(dve, chain_sem, (CH + TOP) * b + CH)
                dve.wait_ge(logit_made, b + 1)
                dve.tensor_tensor(tiles["logits"][:, :, :], ps_t[:, 0, 0:NT * E1].rearrange("p (t e) -> p t e", e=E1),
                                  bg[:, :, :].broadcast_to([P, NT, E1]), ALU.add).then_inc(logit_taken, 1)
                hold(dve, logit_taken, b + 1)
                hold(dve, gt_made, b)
                emit_top2(dve, step, tiles, gap_made, exp_made, b, gates[:, :, :])
                dve.sem_inc(gates_made, 1)

            def take_gates(b):
                dve.wait_ge(gt_made, b + 1)
                dve.tensor_copy(gates_t[:, :], ps_t[0:E1, 1, :]).then_inc(gt_taken, 1)

            def unit(b, more):
                if more:
                    stats_of(b + 1)
                for q in range(NQ):
                    dve.wait_ge(e_made, NQ * b + q + 1)
                    dve.wait_ge(gelu_made, NQ * b + q + 1)
                    if q == 0:
                        after(dve, y_made, 2 * b)
                    dve.tensor_tensor(hid_g[:, q, :], hid[:, q, :], ps_e[:, q % 2, :], ALU.mult).then_inc(gated, 1)
                if more:
                    gating(b + 1)
                for k in range(2):
                    dve.wait_ge(y_made, 2 * b + k + 1)
                    dve.wait_ge(res_loaded, 16 * (b + 1))
                    after(dve, out_stored, 16 * b)
                    dve.scalar_tensor_tensor(y_out[:, 2 * k:2 * k + 2, :], ps_y[:, k, :].rearrange("p (t d) -> p t d", d=D),
                                             gate2[:, 0:1], res[:, 2 * k:2 * k + 2, :], ALU.mult, ALU.add).then_inc(y_taken, 1)
                if more:
                    take_gates(b + 1)

            stats_of(0)
            gating(0)
            take_gates(0)
            unit(0, True)
            with dve.Fori(1, B - 1) as b:
                unit(b, True)
            unit(B - 1, False)


_OUTS = [((B, S, D), "float32")]


def build(nc, ins, outs):
    out = outs[0]
    x1, h0, h, x2, x3 = (nc.dram_tensor(name, [B, S, D], F32) for name in ("x1", "h0", "h", "x2", "x3"))

    def cross(layer, x, to, mask):
        w = lambda kind: [ins[f"L{layer}_xattn_{kind}{m}"] for m in "qkvo"]
        build_attention(nc, f"cross{layer}", dict(
            x=x, ctx=ins["ctx_1024"], mask=mask, res=x, out=to, gate=ins["g_xattn"][layer:layer + 1],
            w=w("W"), bias=w("b")))

    stage_sems = range(min(nc.free_semaphores), max(nc.free_semaphores) + 1)

    def next_stage():
        nc.all_engine_barrier(sems_to_clear=stage_sems)

    cross(0, ins["x"], x1, ins["mask_BxS2_bf1"])
    next_stage()
    build_attention(nc, "self", dict(
        x=x1, ctx=None, mask=None, res=h0, out=h, gate=None, w=[ins[f"L0_ffn_w{m}"] for m in "qkvo"],
        ln_w=ins["L0_ffn_ln1_w"]))
    next_stage()
    build_swiglu_moe(nc, "swiglu", dict(
        x=x1, h=h, out=x2, gate=ins["g_ffn"][0:1], ln_w=ins["L0_ffn_ln2_w"], gate_w=ins["L0_ffn_gate_w"],
        w1=ins["L0_ffn_w1"], w2=ins["L0_ffn_w2"], w3=ins["L0_ffn_w3"]))
    next_stage()
    cross(1, x2, x3, None)
    next_stage()
    build_lora_moe(nc, "lora", dict(
        x=x3, out=out, gate=ins["g_ffn"][1:2], wg=ins["L1_ffn_Wg"], bg=ins["L1_ffn_bg"],
        w1=ins["L1_ffn_W1"], w2=ins["L1_ffn_W2"]))


def kernel(**inputs):
    import numpy as np
    import concourse.bacc as bacc
    from concourse.bass_utils import run_bass_kernel_spmd

    nc = bacc.Bacc("TRN2", target_bir_lowering=False, num_devices=1)
    arrays, ins = {}, {}
    for name, value in inputs.items():
        value = np.ascontiguousarray(np.asarray(value))
        dt = U8 if value.dtype == np.bool_ else mybir.dt.from_np(value.dtype)
        arrays[f"in_{name}_dram"] = value
        ins[name] = nc.dram_tensor(f"in_{name}_dram", value.shape, dt, kind="ExternalInput").ap()
    outs = [nc.dram_tensor(f"out_{i}_dram", shape, mybir.dt.from_np(np.dtype(dtype)), kind="ExternalOutput").ap()
            for i, (shape, dtype) in enumerate(_OUTS)]
    build(nc, ins, outs)
    result = run_bass_kernel_spmd(nc, [arrays], core_ids=[0])
    return result.results[0]["out_0_dram"]
```

```python
from contextlib import ExitStack

import concourse.bass as bass
from concourse import mybir

P = 128
F32 = mybir.dt.float32
F32R = mybir.dt.float32r
U8 = mybir.dt.uint8
U32 = mybir.dt.uint32
I32 = mybir.dt.int32
ALU = mybir.AluOpType
ACT = mybir.ActivationFunctionType
AX = mybir.AxisListType

B, S, D = 8, 512, 256
H, HD = 16, 16
NT = S // P
NC = D // P
GH = 4
NG = H // GH
VW = 32
EPS = 1e-5
SCALE = float(HD) ** -0.5
MASKED = -1e8 / SCALE
RSQRT_SEED = 0x5F3759DF
ONE_ROW = 64
MAX_ROW = 126


def after(eng, sem, count):
    if not isinstance(count, int) or count > 0:
        eng.wait_ge(sem, count)


def hold(eng, sem, count):
    if not isinstance(count, int) or count > 0:
        eng.wait_ge(sem, count)
        eng.nop(nofuse=True)


def emit_rsqrt(dve, step, out, val, tmp):
    step(dve.tensor_scalar(tmp.bitcast(U32), val.bitcast(U32), 1, None, ALU.logical_shift_right))
    step(dve.tensor_scalar(out.bitcast(I32), tmp.bitcast(I32), -1.0, float(RSQRT_SEED), ALU.mult, ALU.add))
    for _ in range(3):
        step(dve.tensor_tensor(tmp, out, out, ALU.mult))
        step(dve.scalar_tensor_tensor(tmp, tmp, -0.5, val, ALU.mult, ALU.mult))
        step(dve.scalar_tensor_tensor(out, tmp, 1.5, out, ALU.add, ALU.mult))


def piece_table(cross):
    if cross:
        table = [((0, 0), "C", 2), ((0, 1), "N", -1), ((0, 1), "C", 3), ((0, 2), "O", -3), ((0, 3), "K", 2),
                 ((1, 0), "K", 3), ((1, 1), "N", 0), ((1, 1), "T", 2), ((1, 2), "O", -2), ((1, 2), "T", 3),
                 ((1, 3), "Q", 2), ((2, 0), "Q", 3), ((2, 1), "N", 1), ((2, 1), "V", 2), ((2, 2), "O", -1),
                 ((2, 3), "OT", -2), ((2, 3), "OT", -1), ((3, 0), "V", 3)]
    else:
        table = [((0, 1), "N", -1), ((0, 2), "O", -3), ((1, 1), "N", 0), ((1, 1), "T", 2), ((1, 2), "O", -2),
                 ((1, 2), "T", 3), ((1, 3), "Q", 2), ((2, 0), "K", 2), ((2, 1), "N", 1), ((2, 1), "Q", 3),
                 ((2, 2), "O", -1), ((2, 2), "K", 3), ((2, 3), "OT", -2), ((2, 3), "OT", -1), ((3, 0), "V", 2),
                 ((3, 0), "V", 3)]
    table += [((3, 1), "N", 2), ((3, 1), "Y", -2), ((3, 2), "Y", -1), ((3, 3), "O", 0)]
    return [(at, kind, off, i % 2) for i, (at, kind, off) in enumerate(table)]


STEPS = 4
MAX_BANK = [i % 3 for i in range(15)] + [1]
MAX_BACK = [min(back for back in range(1, 17) if MAX_BANK[(i - back) % 16] == MAX_BANK[i]) for i in range(16)]
PER = {"T": 2, "C": 2, "Q": 2, "K": 2, "V": 2, "OT": 2, "Y": 2, "N": NG, "O": NG}
PREP = ("T", "C", "Q", "K", "V")


def build_attention(nc, tag, cfg):
    cross, masked = cfg["ctx"] is not None, cfg["mask"] is not None
    src, ctx_d, res_d, out_d = cfg["x"], cfg["ctx"], cfg["res"], cfg["out"]
    table = piece_table(cross)

    with ExitStack() as stack:
        def sb(name, shape, dt=F32):
            return stack.enter_context(nc.sbuf_tensor(f"{tag}_{name}", shape, dt))

        def ps(name, shape):
            return stack.enter_context(nc.psum_tensor(f"{tag}_{name}", shape, F32))

        def sem(name):
            return stack.enter_context(nc.semaphore(f"{tag}_{name}"))

        parts = nc.dram_tensor(f"{tag}_parts", [B, 2, 2, D, S], F32)
        fill = nc.dram_tensor(f"{tag}_fill", [B, 2, S], F32) if masked else None

        ident = sb("ident", [P, P])
        w_raw = sb("w_raw", [P, 4, NC, D])
        w_t = sb("w_t", [P, 4, NC, D])
        bias_col = sb("bias_col", [P, 2, NC])
        bias_row = sb("bias_row", [P, 2, D])
        gate = sb("gate", [P, 1])
        x_in = sb("x_in", [P, NT, D])
        c_in = sb("c_in", [P, NT, D]) if cross else None
        stats = sb("stats", [P, NT, 6])
        mean_var = sb("mean_var", [P, NT, 2])
        small = sb("small", [P, 6, NT])
        x_norm = sb("x_norm", [P, NT, D])
        h0 = None if cross else sb("h0", [P, NT, D])
        x_t = sb("x_t", [P, NC, S])
        c_t = sb("c_t", [P, NC, S]) if cross else x_t
        qk_full = sb("qk_full", [P, 2, NC, S])
        qk_parts = sb("qk_parts", [P, 2, 2, NC, S], F32R)
        q_stack = sb("q_stack", [P, H, S], F32R)
        k_stack = sb("k_stack", [P, H, S], F32R)
        row_pattern = sb("row_pattern", [P - ONE_ROW, 2, S])
        v_new = sb("v_new", [P, NT, D])
        v_aug = sb("v_aug", [P, NT, H, VW])
        probs = sb("probs", [P, NT, GH, S])
        neg_max = sb("neg_max", [P, NT, GH])
        max_parts = sb("max_parts", [P, NT, 2, GH], F32R)
        max_rows = sb("max_rows", [2 * GH, S], F32R)
        o_raw = sb("o_raw", [P, S])
        rec = sb("rec", [P, NT, GH])
        o_tok = sb("o_tok", [P, NT, D])
        o_t = sb("o_t", [P, NC, S])
        res = sb("res", [P, NT, D])
        y_tmp = sb("y_tmp", [P, 2, D])
        y_out = sb("y_out", [P, NT, D])
        mask_b = sb("mask_b", [P, S], U8) if masked else None
        mask_r = sb("mask_r", [B, S], U8) if masked else None
        fill_f = sb("fill_f", [B, S]) if masked else None
        fill_p = sb("fill_p", [B, 2, S], F32R) if masked else None

        ps_max = ps("ps_max", [P, 3, S])
        ps_exp = ps("ps_exp", [P, 2, S])
        ps_pv = ps("ps_pv", [P, S])
        ps_x = ps("ps_x", [P, 2, S])

        w_loaded, ident_made, w_turned, w_taken, gate_made = (sem(n) for n in (
            "w_loaded", "ident_made", "w_turned", "w_taken", "gate_made"))
        fill_chain, fill_stored, pattern_set, rows_set, v_set = (sem(n) for n in (
            "fill_chain", "fill_stored", "pattern_set", "rows_set", "v_set"))
        x_loaded, c_loaded, res_loaded, y_stored, h0_stored = (sem(n) for n in (
            "x_loaded", "c_loaded", "res_loaded", "y_stored", "h0_stored"))
        parts_stored = [sem(f"parts_stored{c}") for c in range(NC)]
        stack_loaded = [sem(f"stack_loaded{g}") for g in range(NG)]
        max_loaded = [sem(f"max_loaded{g}") for g in range(NG)]
        dve_chain = sem("dve_chain")
        x_normed, h0_made = sem("x_normed"), sem("h0_made")
        qk_scored, maxed, max_split = sem("qk_scored"), sem("maxed"), sem("max_split")
        kq_scored, exped, pv_done, pv_taken = sem("kq_scored"), sem("exped"), sem("pv_done"), sem("pv_taken")
        low_made, v_copied = sem("low_made"), sem("v_copied")
        made = {k: sem(f"made_{k}") for k in PER}
        taken = {k: sem(f"taken_{k}") for k in PER}
        done_y, rec_made, max_high = sem("done_y"), sem("rec_made"), sem("max_high")

        W_DMAS = 4 + (1 if not cross else 5) + (1 if masked else 0)
        NEWTON = 11
        norms = 1 if cross else 2
        CHAIN = NT + 1 + norms + NEWTON
        K_BY_DVE = masked

        def has(unit, at, kind, off):
            if kind in PREP:
                return unit in ("first", "mid")
            if unit == "first":
                return kind in ("N", "O") and off >= 0
            if unit == "tail":
                return kind in ("OT", "Y") or off < 0
            return True

        def pieces(unit, s, kt):
            return [(kind, off, bank) for at, kind, off, bank in table if at == (s, kt) and has(unit, at, kind, off)]

        def number(kind, off, b):
            return PER[kind] * b + off

        block = stack.enter_context(nc.Block())

        @block.sync
        def _(sp):
            def load_x(b):
                after(sp, x_normed, NT * b)
                if not cross:
                    after(sp, h0_made, NT * b)
                sp.dma_start(x_in[:, :, :], src[b].rearrange("(t p) d -> p t d", p=P)).then_inc(x_loaded, 16)

            def load_context(b):
                hold(sp, made["C"], 2 * b)
                if masked:
                    hold(sp, taken["K"], 2 * b)
                    sp.dma_start(mask_b[:, :], cfg["mask"][bass.ds(b, 1), :].broadcast_to([P, S])).then_inc(c_loaded, 16)
                sp.dma_start(c_in[:, :, :], ctx_d[b].rearrange("(t p) d -> p t d", p=P)).then_inc(c_loaded, 16)

            def store_h0(b):
                sp.wait_ge(h0_made, NT * b + NT)
                sp.dma_start(res_d[b].rearrange("(t p) d -> p t d", p=P), h0[:, :, :]).then_inc(h0_stored, 16)

            def store_parts(b, c):
                hold(sp, low_made, 4 * b + 2 * c + 2)
                for op in range(2):
                    for part in range(2):
                        sp.dma_start(parts[b, op, part, c * P:c * P + P, :], qk_parts[:, op, part, c, :].bitcast(F32)
                                     ).then_inc(parts_stored[c], 16)

            def load_stack(b, g):
                hold(sp, kq_scored, 16 * (NG * (b - 1) + g + 1))
                sp.wait_ge(parts_stored[g * NC // NG], 64 * (b + 1))
                heads = slice(GH * g, GH * g + GH)
                for op, dst, order in ((0, q_stack, (0, 0, 1, 1)), (1, k_stack, (0, 1, 0, 1))):
                    for row, part in enumerate(order):
                        sp.dma_start(dst[HD * row:HD * row + HD, heads, :].bitcast(F32),
                                     parts[b, op, part, 64 * g:64 * g + 64, :].rearrange("(h d) c -> d h c", d=HD)
                                     ).then_inc(stack_loaded[g], 16)
                if masked:
                    sp.dma_start(k_stack[ONE_ROW:ONE_ROW + 2, heads, :].bitcast(F32),
                                 fill[b].rearrange("r (o c) -> r o c", o=1).broadcast_to([2, GH, S])
                                 ).then_inc(stack_loaded[g], 16)

            def load_res(b):
                if not cross:
                    hold(sp, h0_stored, 16 * (b + 1))
                after(sp, done_y, 2 * b)
                sp.dma_start(res[:, :, :], res_d[b].rearrange("(t p) d -> p t d", p=P)).then_inc(res_loaded, 16)

            def store_y(b):
                sp.wait_ge(done_y, 2 * b + 2)
                sp.dma_start(out_d[b].rearrange("(t p) d -> p t d", p=P), y_out[:, :, :]).then_inc(y_stored, 16)

            def unit(b, kind, more=False):
                for s in range(NG):
                    if kind in ("mid", "last") and s < NG - 1:
                        load_stack(b, s + 1)
                    if s == 0 and kind != "first":
                        load_res(b - 1)
                    if s == 2 and more:
                        load_x(b + 2)
                        if cross:
                            load_context(b + 2)
                    if s == 2 and kind in ("first", "mid") and not cross:
                        store_h0(b + 1)
                    if s > 0 and kind != "tail":
                        if s >= 2 and kind in ("first", "mid"):
                            if s == 3:
                                load_stack(b + 1, 0)
                            store_parts(b + 1, s - 2)
                        if s == 3 and kind != "first":
                            store_y(b - 1)
                if kind == "tail":
                    store_y(b - 1)

            sp.dma_start(x_in[:, :, :], src[0].rearrange("(t p) d -> p t d", p=P)).then_inc(x_loaded, 16)
            for i, w in enumerate(cfg["w"]):
                sp.dma_start(w_raw[:, i], w.rearrange("(o p) i -> p o i", p=P)).then_inc(w_loaded, 16)
            if cross:
                sp.dma_start(gate[:, :], cfg["gate"].rearrange("(o n) -> o n", o=1).broadcast_to([P, 1])).then_inc(w_loaded, 16)
                with nc.allow_non_contiguous_dma(reason="a bias as columns, once"):
                    for i in range(2):
                        sp.dma_start(bias_col[:, i], cfg["bias"][i].rearrange("(g p) -> p g", p=P)).then_inc(w_loaded, 16)
                for i in range(2):
                    sp.dma_start(bias_row[:, i], cfg["bias"][2 + i].rearrange("(o n) -> o n", o=1).broadcast_to([P, D])
                                 ).then_inc(w_loaded, 16)
            else:
                with nc.allow_non_contiguous_dma(reason="a weight as columns, once"):
                    sp.dma_start(bias_col[:, 0], cfg["ln_w"].rearrange("(g p) -> p g", p=P)).then_inc(w_loaded, 16)
            if masked:
                sp.dma_start(mask_r[:, :], cfg["mask"]).then_inc(w_loaded, 16)
                sp.dma_start(mask_b[:, :], cfg["mask"][0:1, :].broadcast_to([P, S])).then_inc(c_loaded, 16)
            if cross:
                sp.dma_start(c_in[:, :, :], ctx_d[0].rearrange("(t p) d -> p t d", p=P)).then_inc(c_loaded, 16)
            sp.wait_ge(pattern_set, 4)
            for i, rows in enumerate((q_stack, k_stack)):
                sp.dma_start(rows[ONE_ROW:P, :, :].bitcast(F32),
                             row_pattern[:, i:i + 1, :].broadcast_to([P - ONE_ROW, H, S])).then_inc(rows_set, 16)
            if masked:
                sp.wait_ge(fill_chain, 3)
                sp.dma_start(fill[:, :, :], fill_p[:, :, :].bitcast(F32)).then_inc(fill_stored, 16)
                sp.wait_ge(fill_stored, 16)
            if not cross:
                store_h0(0)
            sp.wait_ge(rows_set, 32)
            load_x(1)
            if cross:
                load_context(1)
            for c in range(NC):
                store_parts(0, c)
                for g in range(NG // NC * c, NG // NC * (c + 1)):
                    load_stack(0, g)
            unit(0, "first", more=True)
            unit(1, "mid", more=True)
            with sp.Fori(2, B - 2) as b:
                unit(b, "mid", more=True)
            unit(B - 2, "mid")
            unit(B - 1, "last")
            unit(B, "tail")
            sp.wait_ge(y_stored, 16 * B)

        @block.gpsimd
        def _(pool):
            def norm(b):
                pool.wait_ge(dve_chain, CHAIN * (b + 1))
                hold(pool, made["T"], 2 * b)
                factor = 1 + norms
                for t in range(NT):
                    pool.tensor_scalar(x_norm[:, t, :], x_in[:, t, :], mean_var[:, t, 0:1],
                                       small[:, factor, t:t + 1], ALU.subtract, ALU.mult).then_inc(x_normed, 1)
                if not cross:
                    hold(pool, h0_stored, 16 * b)
                    for t in range(NT):
                        pool.tensor_scalar(h0[:, t, :], x_in[:, t, :], mean_var[:, t, 0:1],
                                           small[:, 2, t:t + 1], ALU.subtract, ALU.mult).then_inc(h0_made, 1)

            def low(b, g):
                for op, kind in ((0, "Q"), (1, "K")):
                    pool.wait_ge(taken[kind], 2 * b + g + 1)
                    after(pool, parts_stored[g], 64 * b)
                    pool.tensor_tensor(qk_parts[:, op, 1, g, :], qk_full[:, op, g, :],
                                       qk_parts[:, op, 0, g, :].bitcast(F32), ALU.subtract).then_inc(low_made, 1)

            def copy_v(b, g):
                pool.wait_ge(taken["V"], 2 * b + 2)
                hold(pool, pv_done, NT * (NG * (b - 1) + g + 1))
                pool.tensor_copy(v_aug[:, :, GH * g:GH * g + GH, 0:HD],
                                 v_new[:, :, 64 * g:64 * g + 64].rearrange("p t (h d) -> p t h d", d=HD)
                                 ).then_inc(v_copied, 1)

            def unit(b, kind):
                for s in range(NG):
                    if kind in ("mid", "last") and s < NG - 1:
                        copy_v(b, s + 1)
                    if kind in ("first", "mid"):
                        if s == 0:
                            norm(b + 1)
                        if s == 2:
                            low(b + 1, 0)
                            low(b + 1, 1)
                        if s == 3:
                            copy_v(b + 1, 0)

            pool.memset(ident[:, :], 0.0).then_inc(ident_made, 1)
            pool.wait_ge(ident_made, 1)
            pool.affine_select(out=ident[:, :], in_=ident[:, :], compare_op=ALU.not_equal, fill=1.0, base=0,
                               pattern=[[-1, P]], channel_multiplier=1).then_inc(ident_made, 1)
            norm(0)
            pool.memset(v_aug[:, :, :, :], 0.0).then_inc(v_set, 1)
            pool.wait_ge(v_set, 1)
            pool.memset(v_aug[:, :, :, HD:HD + 1], 1.0).then_inc(v_set, 1)
            low(0, 0)
            low(0, 1)
            for g in range(NG):
                copy_v(0, g)
            unit(0, "first")
            with pool.Fori(1, B - 1) as b:
                unit(b, "mid")
            unit(B - 1, "last")

        @block.tensor
        def _(pe):
            def piece_step(kind, off, bank, b, before, k):
                n = number(kind, off, b)
                out = ps_x[:, bank, :]
                c = off % 2
                if k == 0 and before is not None:
                    pk, poff = before
                    after(pe, taken[pk], number(pk, poff, b) + 1)
                tile = slice(k * P, k * P + P)
                if kind == "T":
                    if k == 0:
                        pe.wait_ge(x_normed, NT * (b + 1) + NT)
                    last = pe.transpose(out[:, tile], x_norm[:, k, c * P:c * P + P], ident[:, :])
                elif kind == "C":
                    if k == 0:
                        pe.wait_ge(c_loaded, (32 if masked else 16) * (b + 2))
                    last = pe.transpose(out[:, tile], c_in[:, k, c * P:c * P + P], ident[:, :])
                elif kind in ("Q", "K"):
                    from_t, w = (x_t, 0) if kind == "Q" else (c_t, 1)
                    if k == 0:
                        pe.wait_ge(taken["C" if cross and kind == "K" else "T"], 2 * (b + 1) + 2)
                    half, i = slice(k // 2 * D, k // 2 * D + D), k % 2
                    last = pe.matmul(out[:, half], w_t[:, w, i, c * P:c * P + P], from_t[:, i, half], start=(i == 0), stop=(i == NC - 1))
                elif kind == "N":
                    if k == 0:
                        pe.wait_ge(max_split, n + 1)
                    last = pe.transpose(out[0:2 * GH, tile], max_parts[:, k].rearrange("p r h -> p (r h)").bitcast(F32), ident[:, :])
                elif kind == "O":
                    if k == 0:
                        pe.wait_ge(pv_taken, n + 1)
                    last = pe.transpose(out[:, tile], o_raw[:, tile], ident[:, :])
                elif kind == "OT":
                    if k == 0:
                        pe.wait_ge(taken["O"], NG * b)
                    last = pe.transpose(out[:, tile], o_tok[:, k, c * P:c * P + P], ident[:, :])
                else:
                    from_t, w = (c_t, 2) if kind == "V" else (o_t, 3)
                    if kind == "Y" and k == 0:
                        pe.wait_ge(taken["OT"], 2 * (b - 1) + 2)
                    t, i = 2 * c + k // 2, k % 2
                    last = pe.matmul(out[:, k // 2 * D:k // 2 * D + D], from_t[:, i, t * P:t * P + P],
                                     w_t[:, w, i, :], start=(i == 0), stop=(i == NC - 1))
                if k == STEPS - 1:
                    last.then_inc(made[kind], 1)

            def score_max(b, s, i):
                n = 16 * (NG * b + s) + i
                if i == 0:
                    pe.wait_ge(stack_loaded[s], (144 if masked else 128) * (b + 1))
                after(pe, maxed, n + 1 - MAX_BACK[i])
                h, t = GH * s + i // NT, i % NT
                pe.matmul(ps_max[:, MAX_BANK[i], :], q_stack[0:MAX_ROW, h, t * P:t * P + P], k_stack[0:MAX_ROW, h, :],
                          start=True, stop=True).then_inc(qk_scored, 1)

            def score_exp(b, s, kt, j):
                ge = (s - 2) % NG
                n = 16 * (NG * b + s - 2) + GH * kt + j
                if kt == 0 and j == 0:
                    pe.wait_ge(max_loaded[ge], 32 * (b + 1 if s >= 2 else b))
                after(pe, exped, n - 1)
                h = GH * ge + j
                pe.matmul(ps_exp[:, j % 2, :], k_stack[:, h, kt * P:kt * P + P], q_stack[:, h, :],
                          start=True, stop=True).then_inc(kq_scored, 1)

            def weigh(b, s, kt):
                g = s % NG
                n = NG * b + s
                pe.wait_ge(exped, 16 * n + GH * (kt + 1))
                if kt == 0:
                    pe.wait_ge(v_copied, n + 1)
                    after(pe, pv_taken, n)
                for j in range(GH):
                    last = pe.matmul(ps_pv[VW * j:VW * j + VW, :], v_aug[:, kt, GH * g + j, :],
                                     probs[:, kt, j, :], start=(kt == 0), stop=(kt == NT - 1),
                                     tile_position=(0, VW * j))
                last.then_inc(pv_done, 1)

            def unit(b, kind, before):
                before = dict(before)
                for s in range(NG):
                    for kt in range(NT):
                        steps = [(p, k) for p in pieces(kind, s, kt) for k in range(STEPS)]
                        share = len(steps) // GH
                        for j in range(GH):
                            if kind != "tail":
                                score_max(b, s, GH * kt + j)
                            if (kind != "first" or s >= 2) and (kind != "tail" or s < 2):
                                score_exp(b, s, kt, j)
                            if j == 1:
                                if kt == 0:
                                    if (kind != "first" or s >= 3) and (kind != "tail" or s < 3):
                                        weigh(b, s - 3, NT - 1)
                                elif (kind != "first" or s >= 2) and (kind != "tail" or s < 2):
                                    weigh(b, s - 2, kt - 1)
                            for (what, off, bank), k in steps[j * share:j * share + share]:
                                piece_step(what, off, bank, b, before[bank], k)
                                if k == STEPS - 1:
                                    before[bank] = (what, off)
                return before

            pe.wait_ge(ident_made, 2)
            pe.wait_ge(w_loaded, 16 * W_DMAS)
            for i in range(8):
                m, c = i // NC, i % NC
                after(pe, w_taken, i - 1)
                for o in range(NC):
                    last = pe.transpose(ps_x[:, i % 2, o * P:o * P + P], w_raw[:, m, o, c * P:c * P + P], ident[:, :])
                last.then_inc(w_turned, 1)
            pe.wait_ge(w_taken, 8)
            before = {0: None, 1: None}
            for _, what, off, bank in table:
                if what in PREP:
                    for k in range(STEPS):
                        piece_step(what, off, bank, -1, before[bank], k)
                    before[bank] = (what, off)
            def next_unit(before):
                return {bank: (what, off - PER[what]) for bank, (what, off) in before.items()}

            pe.wait_ge(rows_set, 32)
            pe.wait_ge(v_set, 2)
            before = {bank: (what, off - 2) for bank, (what, off) in before.items()}
            before = next_unit(unit(0, "first", before))
            before = next_unit(unit(1, "mid", before))
            with pe.Fori(2, B - 1) as b:
                unit(b, "mid", before)
            before = next_unit(unit(B - 1, "last", before))
            unit(B, "tail", before)

        @block.scalar
        def _(act):
            def take(kind, off, bank, b):
                n = number(kind, off, b)
                c = off % 2
                got = ps_x[:, bank, :]
                if kind == "T":
                    act.wait_ge(made[kind], n + 1)
                    if cross:
                        act.activation(x_t[:, c, :], got, ACT.Copy).then_inc(taken[kind], 1)
                    else:
                        act.activation(x_t[:, c, :], got, ACT.Identity, scale=bias_col[:, 0, c:c + 1]).then_inc(taken[kind], 1)
                elif kind == "C":
                    act.wait_ge(made[kind], n + 1)
                    act.activation(c_t[:, c, :], got, ACT.Copy).then_inc(taken[kind], 1)
                elif kind == "Q" or (kind == "K" and not K_BY_DVE):
                    op = 0 if kind == "Q" else 1
                    act.wait_ge(made[kind], n + 1)
                    after(act, low_made, 4 * (b + 1))
                    after(act, parts_stored[c], 64 * (b + 1))
                    bias = bias_col[:, op, c:c + 1] if cross else 0.0
                    act.activation(qk_full[:, op, c, :], got, ACT.Identity, bias=bias)
                    act.activation(qk_parts[:, op, 0, c, :], got, ACT.Identity, bias=bias).then_inc(taken[kind], 1)
                elif kind == "N":
                    act.wait_ge(made[kind], n + 1)
                    after(act, max_loaded[(off - 1) % NG], 32 * (b + 1 if off >= 1 else b))
                    act.activation(max_rows[:, :], got[0:2 * GH, :], ACT.Copy).then_inc(taken[kind], 1)
                elif kind == "OT":
                    act.wait_ge(made[kind], n + 1)
                    act.activation(o_t[:, c, :], got, ACT.Copy).then_inc(taken[kind], 1)

            def exp(b, s, kt, j):
                n = 16 * (NG * b + s - 2) + GH * kt + j
                act.wait_ge(kq_scored, n + 1)
                if j == 0:
                    after(act, pv_done, NT * (NG * b + s - 3) + kt + 1)
                act.activation(probs[:, kt, j, :], ps_exp[:, j % 2, :], ACT.Exp, scale=SCALE).then_inc(exped, 1)

            def load_max(b, s):
                g = (s - 1) % NG
                hold(act, taken["N"], NG * b + s)
                for part in range(2):
                    act.dma_start(q_stack[MAX_ROW + part:MAX_ROW + part + 1, GH * g:GH * g + GH, :].bitcast(F32),
                                 max_rows[GH * part:GH * part + GH, :].bitcast(F32)).then_inc(max_loaded[g], 16)

            def take_pv(b, s):
                n = NG * b + s
                act.wait_ge(pv_done, NT * n + NT)
                after(act, made["O"], n)
                act.activation(o_raw[:, :], ps_pv[:, :], ACT.Copy).then_inc(pv_taken, 1)

            def unit(b, kind):
                for s in range(NG):
                    for kt in range(NT):
                        if kt == 2 and (kind != "first" or s > 0) and (kind != "tail" or s == 0):
                            load_max(b, s)
                        got = pieces(kind, s, kt)
                        early = got[:1] if len(got) == 2 else []
                        for j in range(GH):
                            if (kind != "first" or s >= 2) and (kind != "tail" or s < 2):
                                exp(b, s, kt, j)
                            if j == 2:
                                for what, off, bank in early:
                                    take(what, off, bank, b)
                        if kt == 0 and (kind != "first" or s >= 3) and (kind != "tail" or s < 3):
                            take_pv(b, s - 3)
                        for what, off, bank in got[len(early):]:
                            take(what, off, bank, b)

            act.wait_ge(w_loaded, 16 * W_DMAS)
            if cross:
                act.activation(gate[:, :], gate[:, :], ACT.Tanh).then_inc(gate_made, 1)
            for i in range(8):
                act.wait_ge(w_turned, i + 1)
                act.activation(w_t[:, i // NC, i % NC, :], ps_x[:, i % 2, 0:D], ACT.Copy).then_inc(w_taken, 1)
            for _, what, off, bank in table:
                if what in PREP:
                    take(what, off, bank, -1)
            unit(0, "first")
            with act.Fori(1, B - 1) as b:
                unit(b, "mid")
            unit(B - 1, "last")
            unit(B, "tail")

        @block.vector
        def _(dve):
            def rsqrt_step(k, out, val, tmp):
                if k == 0:
                    return dve.tensor_scalar(tmp.bitcast(U32), val.bitcast(U32), 1, None, ALU.logical_shift_right)
                if k == 1:
                    return dve.tensor_scalar(out.bitcast(I32), tmp.bitcast(I32), -1.0, float(RSQRT_SEED), ALU.mult, ALU.add)
                if k % 3 == 2:
                    return dve.tensor_tensor(tmp, out, out, ALU.mult)
                if k % 3 == 0:
                    return dve.scalar_tensor_tensor(tmp, tmp, -0.5, val, ALU.mult, ALU.mult)
                return dve.scalar_tensor_tensor(out, tmp, 1.5, out, ALU.add, ALU.mult)

            def stats_step(b, k):
                if k < NT:
                    if k == 0:
                        dve.wait_ge(x_loaded, 16 * (b + 1))
                        after(dve, x_normed, NT * b)
                        if not cross:
                            after(dve, h0_made, NT * b)
                    dve.bn_stats(stats[:, k, :], x_in[:, k, :]).then_inc(dve_chain, 1)
                    return
                k -= NT - 1
                if k == 1:
                    hold(dve, dve_chain, CHAIN * b + NT)
                    for t in range(NT):
                        last = dve.bn_aggr(mean_var[:, t, :], stats[:, t, :])
                else:
                    dve.wait_ge(dve_chain, CHAIN * b + NT - 1 + k)
                    if k == 2:
                        last = dve.tensor_scalar(small[:, 0, :], mean_var[:, :, 1], EPS, None, ALU.add)
                    elif k == 3 and not cross:
                        last = dve.scalar_tensor_tensor(small[:, 1, :], small[:, 0, :], EPS, mean_var[:, :, 1], ALU.mult, ALU.add)
                    else:
                        last = rsqrt_step(k - (CHAIN - NEWTON - NT + 1), small[:, 2:2 + norms], small[:, 0:norms], small[:, 4:4 + norms])
                last.then_inc(dve_chain, 1)

            def take(kind, off, bank, b):
                n = number(kind, off, b)
                c = off % 2
                got = ps_x[:, bank, :]
                if kind == "K" and K_BY_DVE:
                    dve.wait_ge(made[kind], n + 1)
                    dve.wait_ge(c_loaded, 32 * (b + 2))
                    after(dve, low_made, 4 * (b + 1))
                    after(dve, parts_stored[c], 64 * (b + 1))
                    for dst in (qk_full[:, 1, c, :], qk_parts[:, 1, 0, c, :]):
                        last = dve.scalar_tensor_tensor(dst, got, bias_col[:, 1, c:c + 1], mask_b[:, :], ALU.add, ALU.mult)
                    last.then_inc(taken[kind], 1)
                elif kind == "V":
                    dve.wait_ge(made[kind], n + 1)
                    after(dve, v_copied, NG * (b + 1))
                    dst = v_new[:, 2 * c:2 * c + 2, :]
                    both = got.rearrange("p (t d) -> p t d", d=D)
                    if cross:
                        dve.tensor_tensor(dst, both, bias_row[:, 0:1, :].broadcast_to([P, 2, D]), ALU.add).then_inc(taken[kind], 1)
                    else:
                        dve.tensor_copy(dst, both).then_inc(taken[kind], 1)
                elif kind == "O":
                    g = off % NG
                    dve.wait_ge(made[kind], n + 1)
                    if off == 0:
                        after(dve, made["OT"], 2 * b)
                    after(dve, taken[kind], n)
                    rows = got.rearrange("p (t h e) -> p t h e", t=NT, e=VW)
                    dve.reciprocal(rec[:, :, :], rows[:, :, :, HD]).then_inc(rec_made, 1)
                    dve.wait_ge(rec_made, n + 1)
                    dve.tensor_tensor(o_tok[:, :, 64 * g:64 * g + 64].rearrange("p t (h d) -> p t h d", d=HD),
                                      rows[:, :, :, 0:HD], rec[:, :, :].rearrange("p t (h o) -> p t h o", o=1).broadcast_to([P, NT, GH, HD]),
                                      ALU.mult).then_inc(taken[kind], 1)
                elif kind == "Y":
                    dve.wait_ge(made[kind], n + 1)
                    dve.wait_ge(res_loaded, 16 * b)
                    after(dve, y_stored, 16 * (b - 1))
                    tiles = slice(2 * c, 2 * c + 2)
                    both = got.rearrange("p (t d) -> p t d", d=D)
                    if cross:
                        after(dve, done_y, n)
                        dve.tensor_tensor(y_tmp[:, :, :], both, bias_row[:, 1:2, :].broadcast_to([P, 2, D]), ALU.add).then_inc(taken[kind], 1)
                        dve.wait_ge(taken[kind], n + 1)
                        dve.scalar_tensor_tensor(y_out[:, tiles, :], y_tmp[:, :, :], gate[:, 0:1], res[:, tiles, :],
                                                 ALU.mult, ALU.add).then_inc(done_y, 1)
                    else:
                        dve.tensor_tensor(y_out[:, tiles, :], both, res[:, tiles, :], ALU.add).then_inc(taken[kind], 1)
                        dve.wait_ge(taken[kind], n + 1)
                        dve.sem_inc(done_y, 1)

            def maxima(b, s, i):
                n = 16 * (NG * b + s) + i
                j, t = i // NT, i % NT
                dve.wait_ge(qk_scored, n + 1)
                dve.tensor_reduce(neg_max[:, t, j:j + 1], ps_max[:, MAX_BANK[i], :], AX.X, ALU.max, negate=True).then_inc(maxed, 1)

            def split_max(b, s):
                n = NG * b + s
                dve.wait_ge(maxed, 16 * n + 16)
                after(dve, made["N"], n)
                dve.tensor_copy(max_parts[:, :, 0, :], neg_max[:, :, :]).then_inc(max_high, 1)
                dve.wait_ge(max_high, n + 1)
                dve.tensor_tensor(max_parts[:, :, 1, :], neg_max[:, :, :], max_parts[:, :, 0, :].bitcast(F32),
                                  ALU.subtract).then_inc(max_split, 1)

            stats_steps = [[i] if i < NT else [k for k in (2 * i - NT, 2 * i - NT + 1) if k < CHAIN] for i in range(16)]

            def unit(b, kind):
                for s in range(NG):
                    for kt in range(NT):
                        got = pieces(kind, s, kt)
                        early = got[:1] if len(got) == 2 else []
                        if kind != "tail":
                            if kt == 0:
                                after(dve, max_split, NG * b + s)
                            for j in range(GH):
                                maxima(b, s, GH * kt + j)
                                if s == 0 and kind in ("first", "mid"):
                                    for k in stats_steps[GH * kt + j]:
                                        stats_step(b + 1, k)
                                if j == 2:
                                    for what, off, bank in early:
                                        take(what, off, bank, b)
                            if kt == NT - 1:
                                split_max(b, s)
                        for what, off, bank in got if kind == "tail" else got[len(early):]:
                            take(what, off, bank, b)

            for i in range(2):
                dve.memset(row_pattern[:, i, :], float(i)).then_inc(pattern_set, 1)
            dve.wait_ge(pattern_set, 2)
            for i in range(2):
                dve.memset(row_pattern[0:2, i, :], float(1 - i)).then_inc(pattern_set, 1)
            if masked:
                dve.wait_ge(w_loaded, 16 * W_DMAS)
                dve.tensor_scalar(fill_f[:, :], mask_r[:, :], -MASKED, MASKED, ALU.mult, ALU.add).then_inc(fill_chain, 1)
                dve.wait_ge(fill_chain, 1)
                dve.tensor_copy(fill_p[:, 0, :], fill_f[:, :]).then_inc(fill_chain, 1)
                dve.wait_ge(fill_chain, 2)
                dve.tensor_tensor(fill_p[:, 1, :], fill_f[:, :], fill_p[:, 0, :].bitcast(F32), ALU.subtract).then_inc(fill_chain, 1)
            for k in range(CHAIN):
                stats_step(0, k)
            dve.wait_ge(w_loaded, 16 * W_DMAS)
            if cross:
                dve.wait_ge(gate_made, 1)
            for _, what, off, bank in table:
                if what in PREP:
                    take(what, off, bank, -1)
            unit(0, "first")
            unit(1, "mid")
            with dve.Fori(2, B - 1) as b:
                unit(b, "mid")
            unit(B - 1, "last")
            unit(B, "tail")

E0, FF = 8, 512
E1, RANK = 8, 64
NF = FF // P
NB = B
PASSES = ((0, 0), (0, 1), (1, 0))


class Chain:

    def __init__(self, dve, sem, start):
        self.dve, self.sem, self.at = dve, sem, start

    def __call__(self, ins, wait=after):
        self.at = self.at + 1
        ins.then_inc(self.sem, 1)
        wait(self.dve, self.sem, self.at)


def emit_top2(dve, step, tiles, made_gap, exp_done, n, out):
    logits, best, where, place, iota, g, one_hot = (
        tiles[k] for k in ("logits", "best", "where", "place", "iota", "g", "one_hot"))
    count = logits.shape[1]
    for t in range(count):
        last = dve.max(best[:, t, :], logits[:, t, :])
    step(last, hold)
    for t in range(count):
        last = dve.max_index(where[:, t, :], best[:, t, :], logits[:, t, :])
    step(last)
    dve.tensor_tensor(g[:, 0, :], best[:, :, 1], best[:, :, 0], ALU.subtract).then_inc(made_gap, 1)
    step(dve.tensor_copy(place[:, :, :], where[:, :, 0:2]))
    for k in range(2):
        last = dve.tensor_tensor(one_hot[:, k], iota[:, :, :].broadcast_to([P, count, 8]),
                                 place[:, :, k:k + 1].broadcast_to([P, count, 8]), ALU.is_equal)
    step(last)
    dve.wait_ge(exp_done, n + 1)
    step(dve.tensor_scalar(g[:, 2, :], g[:, 1, :], 1.0, None, ALU.add))
    step(dve.reciprocal(g[:, 3, :], g[:, 2, :]))
    step(dve.tensor_tensor(g[:, 4, :], g[:, 1, :], g[:, 3, :], ALU.mult))
    for k in range(2):
        last = dve.tensor_tensor(one_hot[:, k], one_hot[:, k],
                                 g[:, 3 + k, :].rearrange("p (t o) -> p t o", o=1).broadcast_to([P, count, 8]), ALU.mult)
    step(last)
    step(dve.tensor_tensor(out, one_hot[:, 0], one_hot[:, 1], ALU.add))


TOP2_STEPS = 9


def top2_tiles(sb, space, count):
    def cut(at, width, shape="p (t e) -> p t e", **sizes):
        return space[0][:, at * count:(at + width) * count].rearrange(shape, **sizes)
    return {
        "logits": cut(0, 8, e=8), "best": cut(8, 8, e=8), "where": cut(16, 8, e=8).bitcast(U32), "place": cut(24, 2, e=2),
        "g": cut(26, 5, "p (k t) -> p k t", k=5),
        "one_hot": space[1][:, 0:16 * count].rearrange("p (k t e) -> p k t e", k=2, e=8), "iota": sb("iota", [P, 1, 8]),
    }


def emit_ident(pool, ident, made):
    pool.memset(ident[:, :], 0.0).then_inc(made, 1)
    pool.wait_ge(made, 1)
    pool.affine_select(out=ident[:, :], in_=ident[:, :], compare_op=ALU.not_equal, fill=1.0, base=0,
                       pattern=[[-1, P]], channel_multiplier=1).then_inc(made, 1)


def by_token(dram, b):
    return dram[b].rearrange("(t p) d -> p t d", p=P)


def build_swiglu_moe(nc, tag, cfg):
    h_d, x_d, out_d = cfg["h"], cfg["x"], cfg["out"]
    with ExitStack() as stack:
        def sb(name, shape, dt=F32):
            return stack.enter_context(nc.sbuf_tensor(f"{tag}_{name}", shape, dt))

        def ps(name, shape):
            return stack.enter_context(nc.psum_tensor(f"{tag}_{name}", shape, F32))

        def sem(name):
            return stack.enter_context(nc.semaphore(f"{tag}_{name}"))

        ident = sb("ident", [P, P])
        ln_col = sb("ln_col", [P, NC])
        gate = sb("gate", [P, 1])
        gw_raw = sb("gw_raw", [E0, D])
        gw_t = sb("gw_t", [P, NC, E0])
        n_tok = [sb(f"n_tok{i}", [P, NT, D]) for i in range(2)]
        mean_var, small = sb("mean_var", [P, NB * NT, 2]), sb("small", [P, 3, NB * NT])
        n_part = [sb(f"n_part{i}", [P, NC, B * S], F32R) for i in range(2)]
        gates = sb("gates", [P, NB * NT, E0])
        acc = sb("acc", [P, NB * NT, D])
        raw13 = sb("raw13", [P, 2, NF, D])
        raw2 = sb("raw2", [P, NC, FF])
        w13 = [[sb(f"w13_{q}{part}", [P, 2, NC, FF], F32R) for part in range(2)] for q in range(2)]
        w2 = [[sb(f"w2_{q}{part}", [P, NF, D], F32R) for part in range(2)] for q in range(2)]
        silu = sb("silu", [P, 2, S])
        hid = sb("hid", [P, 2, S])
        hid_part = [[sb(f"hid_{q}{part}", [P, NF, S], F32R) for part in range(2)] for q in range(2)]

        n_full = (silu, hid)
        spare = [n[:, :, :].rearrange("p t d -> p (t d)") for n in n_tok]
        stats = spare[0][:, 0:6 * NB * NT].rearrange("p (t k) -> p t k", k=6)
        tiles = top2_tiles(sb, spare, NB * NT)

        ps_g = ps("ps_g", [P, 2, S])
        ps_u = ps("ps_u", [P, 2, S])
        ps_y = ps("ps_y", [P, 2, S])
        ps_w = ps("ps_w", [P, 2, S])

        ident_made, const_loaded, gate_made, gw_made, gw_taken, iota_made = (sem(n) for n in (
            "ident_made", "const_loaded", "gate_made", "gw_made", "gw_taken", "iota_made"))
        acc_loaded, chain_sem, normed = (sem(n) for n in ("acc_loaded", "chain", "normed"))
        turned, t_taken, low_made, logit_made, logit_taken, gap_made, exp_made, gates_made = (sem(n) for n in (
            "turned", "t_taken", "low_made", "logit_made", "logit_taken", "gap_made", "exp_made", "gates_made"))
        raw_loaded, w_turned, w_high, w_low = (sem(n) for n in ("raw_loaded", "w_turned", "w_high", "w_low"))
        g_made, u_made, silu_made, hid_made, hid_high, hid_low = (sem(n) for n in (
            "g_made", "u_made", "silu_made", "hid_made", "hid_high", "hid_low"))
        y_made, y_taken = sem("y_made"), sem("y_taken")
        x_loaded = [sem(f"x_loaded{i}") for i in range(2)]
        out_made, out_stored = sem("out_made"), [sem(f"out_stored{i}") for i in range(2)]

        block = stack.enter_context(nc.Block())

        @block.sync
        def _(sp):
            def load_raw(e):
                after(sp, w_turned, 6 * e)
                sp.dma_start(raw13[:, 0], cfg["w1"][e].rearrange("(o p) i -> p o i", p=P)).then_inc(raw_loaded, 16)
                sp.dma_start(raw13[:, 1], cfg["w3"][e].rearrange("(o p) i -> p o i", p=P)).then_inc(raw_loaded, 16)
                sp.dma_start(raw2[:, :, :], cfg["w2"][e].rearrange("(o p) i -> p o i", p=P)).then_inc(raw_loaded, 16)

            load_raw(0)
            sp.dma_start(acc[:, :, :], h_d[:, :, :].rearrange("b (t p) d -> p (b t) d", p=P)).then_inc(acc_loaded, 16)
            with nc.allow_non_contiguous_dma(reason="a weight as columns, once"):
                sp.dma_start(ln_col[:, :], cfg["ln_w"].rearrange("(g p) -> p g", p=P)).then_inc(const_loaded, 16)
            sp.dma_start(gate[:, :], cfg["gate"].rearrange("(o n) -> o n", o=1).broadcast_to([P, 1])).then_inc(const_loaded, 16)
            sp.dma_start(gw_raw[:, :], cfg["gate_w"]).then_inc(const_loaded, 16)
            with sp.Fori(1, E0) as e:
                load_raw(e)
            for i, dst in enumerate(n_tok):
                sp.wait_ge(turned, 2 * NB)
                sp.dma_start(dst[:, :, :], by_token(x_d, i)).then_inc(x_loaded[i], 16)
            for b in range(NB):
                sp.wait_ge(out_made, b + 1)
                sp.dma_start(by_token(out_d, b), acc[:, NT * b:NT * b + NT, :]).then_inc(out_stored[b % 2], 16)
                if b + 2 < NB:
                    sp.dma_start(n_tok[b % 2][:, :, :], by_token(x_d, b + 2)).then_inc(x_loaded[b % 2], 16)
            for i in range(2):
                sp.wait_ge(out_stored[i], 16 * NB // 2)

        @block.gpsimd
        def _(pool):
            emit_ident(pool, ident, ident_made)
            for e in range(E0):
                last = pool.memset(tiles["iota"][:, :, e:e + 1], float(e))
                last.then_inc(iota_made, 1)

            def low_tokens(b, q):
                for c in range(NC):
                    pool.wait_ge(t_taken, 2 * b + c + 1)
                    at = bass.ds(b * S, S)
                    pool.tensor_tensor(n_part[1][:, c, at], n_full[q][:, c, :], n_part[0][:, c, at].bitcast(F32),
                                       ALU.subtract).then_inc(low_made, 1)

            with pool.Fori(0, NB // 2) as pair:
                for q in range(2):
                    low_tokens(2 * pair + q, q)

            with pool.Fori(0, E0 // 2) as pair:
                for q in range(2):
                    for b in range(NB):
                        for f in range(NF):
                            n = (2 * pair + q) * NB * NF + b * NF + f
                            pool.wait_ge(hid_high, n + 1)
                            pool.tensor_tensor(hid_part[b % 2][1][:, f, :], hid[:, f % 2, :],
                                               hid_part[b % 2][0][:, f, :].bitcast(F32), ALU.subtract).then_inc(hid_low, 1)

        def weight_piece(i):
            if i < 4:
                m, c = i // 2, i % 2
                return [raw13[:, m, o, c * P:c * P + P] for o in range(NF)], lambda w: w13[w[0]][w[1]][:, m, c, :]
            f = 2 * (i - 4)
            return ([raw2[:, o, (f + k) * P:(f + k) * P + P] for k in range(2) for o in range(NC)],
                    lambda w: w2[w[0]][w[1]][:, f:f + 2, :].rearrange("p f d -> p (f d)"))

        @block.tensor
        def _(pe):
            def turn_weights(e, i):
                if i == 0:
                    pe.wait_ge(raw_loaded, 48 * (e + 1))
                after(pe, w_low, 6 * e + i - 1)
                for k, blk in enumerate(weight_piece(i)[0]):
                    last = pe.transpose(ps_w[:, i % 2, k * P:k * P + P], blk, ident[:, :])
                last.then_inc(w_turned, 1)

            pe.wait_ge(ident_made, 2)
            pe.wait_ge(const_loaded, 48)
            for c in range(NC):
                last = pe.transpose(ps_y[:, 0, c * E0:c * E0 + E0], gw_raw[:, c * P:c * P + P], ident[0:E0, 0:E0])
            last.then_inc(gw_made, 1)
            for i in range(6):
                turn_weights(0, i)
            pe.wait_ge(gw_taken, 1)
            def turn(b, q):
                pe.wait_ge(normed, b + 1)
                after(pe, t_taken, 2 * b - 2)
                for c in range(NC):
                    for t in range(NT):
                        last = pe.transpose((ps_g, ps_y)[q][:, c, t * P:t * P + P], n_tok[q][:, t, c * P:c * P + P], ident[:, :])
                    last.then_inc(turned, 1)

            def score(b, q):
                pe.wait_ge(t_taken, 2 * b + 2)
                for t in range(NT):
                    for c in range(NC):
                        last = pe.matmul(ps_u[:, 0, bass.ds(b * NT * E0 + t * E0, E0)], n_full[q][:, c, t * P:t * P + P],
                                         gw_t[:, c, :], start=(c == 0), stop=(c == NC - 1))
                last.then_inc(logit_made, 1)

            turn(0, 0)
            turn(1, 1)
            score(0, 0)
            with pe.Fori(0, NB // 2 - 1) as pair:
                turn(2 * pair + 2, 0)
                score(2 * pair + 1, 1)
                turn(2 * pair + 3, 1)
                score(2 * pair + 2, 0)
            score(NB - 1, 1)

            def project(which, dst, free, made_sem, n, q, b, f):
                after(pe, free, n - 1)
                k = 0
                for c in range(NC):
                    for wp, ap in PASSES:
                        last = pe.matmul(dst[:, f % 2, :], w13[q][wp][:, which, c, f * P:f * P + P],
                                         n_part[ap][:, c, b * S:b * S + S], start=(k == 0), stop=(k == 5))
                        k += 1
                last.then_inc(made_sem, 1)

            def down(q, b, t, n):
                if t == 0:
                    pe.wait_ge(hid_low, NF * n + NF)
                after(pe, y_taken, NT * n + t - 1)
                k = 0
                for f in range(NF):
                    for wp, ap in PASSES:
                        last = pe.matmul(ps_y[:, t % 2, 0:D],
                                         hid_part[b % 2][ap][:, f, t * P:t * P + P], w2[q][wp][:, f, :],
                                         start=(k == 0), stop=(k == 3 * NF - 1))
                        k += 1
                last.then_inc(y_made, 1)

            def expert(e, q, first, last_one):
                pe.wait_ge(w_low, 6 * e + 6)
                for b in range(NB):
                    for f in range(NF):
                        n = (e * NB + b) * NF + f
                        project(0, ps_g, silu_made, g_made, n, q, b, f)
                        project(1, ps_u, hid_high, u_made, n, q, b, f)
                        if b > 0:
                            down(q, b - 1, f, e * NB + b - 1)
                        elif not first:
                            down(1 - q, NB - 1, f, e * NB - 1)
                    if b >= 1 and b < 7 and not last_one:
                        turn_weights(e + 1, b - 1)

            pe.wait_ge(low_made, 2 * NB)
            pe.wait_ge(logit_taken, 1)
            expert(0, 0, True, False)
            with pe.Fori(0, E0 // 2 - 1) as pair:
                expert(2 * pair + 1, 1, False, False)
                expert(2 * pair + 2, 0, False, False)
            expert(E0 - 1, 1, False, True)
            for t in range(NT):
                down(1, NB - 1, t, E0 * NB - 1)

        @block.scalar
        def _(act):
            def take_weights(e, q, i):
                act.wait_ge(w_turned, 6 * e + i + 1)
                act.activation(weight_piece(i)[1]((q, 0)), ps_w[:, i % 2, :], ACT.Copy).then_inc(w_high, 1)

            act.wait_ge(const_loaded, 48)
            act.activation(gate[:, :], gate[:, :], ACT.Tanh).then_inc(gate_made, 1)
            for i in range(6):
                take_weights(0, 0, i)
            def take_tokens(b, q):
                after(act, low_made, 2 * b - 2)
                after(act, logit_made, b - 1)
                for c in range(NC):
                    act.wait_ge(turned, 2 * b + c + 1)
                    got = (ps_g, ps_y)[q][:, c, :]
                    act.activation(n_full[q][:, c, :], got, ACT.Identity, scale=ln_col[:, c:c + 1])
                    act.activation(n_part[0][:, c, bass.ds(b * S, S)], got, ACT.Identity,
                                   scale=ln_col[:, c:c + 1]).then_inc(t_taken, 1)

            take_tokens(0, 0)
            take_tokens(1, 1)
            with act.Fori(1, NB // 2) as pair:
                for q in range(2):
                    take_tokens(2 * pair + q, q)
            act.wait_ge(gap_made, 1)
            act.activation(tiles["g"][:, 1, :], tiles["g"][:, 0, :], ACT.Exp).then_inc(exp_made, 1)

            def expert(e, q, last_one):
                for b in range(NB):
                    for f in range(NF):
                        n = (e * NB + b) * NF + f
                        act.wait_ge(g_made, n + 1)
                        after(act, hid_high, n - 1)
                        act.activation(silu[:, f % 2, :], ps_g[:, f % 2, :], ACT.Silu).then_inc(silu_made, 1)
                    if b >= 1 and b < 7 and not last_one:
                        take_weights(e + 1, 1 - q, b - 1)

            act.wait_ge(low_made, 2 * NB)
            act.wait_ge(logit_made, NB)
            expert(0, 0, False)
            with act.Fori(0, E0 // 2 - 1) as pair:
                expert(2 * pair + 1, 1, False)
                expert(2 * pair + 2, 0, False)
            expert(E0 - 1, 1, True)

        @block.vector
        def _(dve):
            def low_weights(e, q, i):
                dve.wait_ge(w_high, 6 * e + i + 1)
                to = weight_piece(i)[1]
                dve.tensor_tensor(to((q, 1)), ps_w[:, i % 2, :], to((q, 0)).bitcast(F32), ALU.subtract).then_inc(w_low, 1)

            dve.wait_ge(gw_made, 1)
            dve.tensor_copy(gw_t[:, :, :].rearrange("p c e -> p (c e)"), ps_y[:, 0, 0:NC * E0]).then_inc(gw_taken, 1)
            for i in range(6):
                low_weights(0, 0, i)
            dve.wait_ge(iota_made, E0)
            step = Chain(dve, chain_sem, 0)
            dve.wait_ge(acc_loaded, 16)
            for t in range(NB * NT):
                last = dve.bn_stats(stats[:, t, :], acc[:, t, :])
            step(last)
            for t in range(NB * NT):
                last = dve.bn_aggr(mean_var[:, t, :], stats[:, t, :])
            step(last)
            step(dve.tensor_tensor(small[:, 2, :], mean_var[:, :, 0], mean_var[:, :, 0], ALU.mult))
            step(dve.scalar_tensor_tensor(small[:, 0, :], small[:, 2, :], EPS, mean_var[:, :, 1], ALU.add, ALU.add))
            emit_rsqrt(dve, step, small[:, 1, :], small[:, 0, :], small[:, 2, :])

            def norm(b, q):
                after(dve, turned, 2 * b - 2)
                for t in range(NT):
                    last = dve.tensor_scalar(n_tok[q][:, t, :], acc[:, b * NT + t, :],
                                             small[:, 1, bass.ds(b * NT + t, 1)], None, ALU.mult)
                last.then_inc(normed, 1)

            norm(0, 0)
            norm(1, 1)
            with dve.Fori(1, NB // 2) as pair:
                for q in range(2):
                    norm(2 * pair + q, q)
            dve.wait_ge(logit_made, NB)
            dve.tensor_copy(tiles["logits"].rearrange("p t e -> p (t e)"), ps_u[:, 0, 0:NB * NT * E0]).then_inc(logit_taken, 1)
            dve.wait_ge(logit_taken, 1)
            emit_top2(dve, step, tiles, gap_made, exp_made, 0, gates[:, :, :])

            def add_tile(n, b, t, e):
                dve.wait_ge(y_made, NT * n + t + 1)
                tile = NT * b + t
                dve.scalar_tensor_tensor(acc[:, tile, :], ps_y[:, t % 2, 0:D],
                                         gates[:, tile, bass.ds(e, 1)], acc[:, tile, :], ALU.mult, ALU.add).then_inc(y_taken, 1)

            def expert(e, q, first, last_one):
                for b in range(NB):
                    for f in range(NF):
                        n = (e * NB + b) * NF + f
                        dve.wait_ge(u_made, n + 1)
                        dve.wait_ge(silu_made, n + 1)
                        after(dve, hid_low, n - 1)
                        if f == 0:
                            after(dve, y_made, NT * (e * NB + b - 1))
                        dve.tensor_tensor(hid[:, f % 2, :], silu[:, f % 2, :], ps_u[:, f % 2, :], ALU.mult)
                        dve.tensor_tensor(hid_part[b % 2][0][:, f, :], silu[:, f % 2, :], ps_u[:, f % 2, :],
                                          ALU.mult).then_inc(hid_high, 1)
                        if b > 0:
                            add_tile(e * NB + b - 1, b - 1, f, e)
                        elif not first:
                            add_tile(e * NB - 1, NB - 1, f, e - 1)
                    if b >= 1 and b < 7 and not last_one:
                        low_weights(e + 1, 1 - q, b - 1)

            dve.wait_ge(low_made, 2 * NB)
            expert(0, 0, True, False)
            with dve.Fori(0, E0 // 2 - 1) as pair:
                expert(2 * pair + 1, 1, False, False)
                expert(2 * pair + 2, 0, False, False)
            expert(E0 - 1, 1, False, True)
            for t in range(NT):
                add_tile(E0 * NB - 1, NB - 1, t, E0 - 1)
            dve.wait_ge(y_taken, E0 * NB * NT)
            dve.wait_ge(gate_made, 1)
            for b in range(NB):
                dve.wait_ge(x_loaded[b % 2], 16 * (b // 2 + 1))
                here = acc[:, NT * b:NT * b + NT, :]
                dve.scalar_tensor_tensor(here, here, gate[:, 0:1], n_tok[b % 2][:, :, :], ALU.mult, ALU.add).then_inc(out_made, 1)


def build_lora_moe(nc, tag, cfg):
    x_d, out_d = cfg["x"], cfg["out"]
    NQ = E1 * RANK // P
    with ExitStack() as stack:
        def sb(name, shape, dt=F32):
            return stack.enter_context(nc.sbuf_tensor(f"{tag}_{name}", shape, dt))

        def ps(name, shape):
            return stack.enter_context(nc.psum_tensor(f"{tag}_{name}", shape, F32))

        def sem(name):
            return stack.enter_context(nc.semaphore(f"{tag}_{name}"))

        ident = sb("ident", [P, P])
        gate = sb("gate", [P, 1])
        gate2 = sb("gate2", [P, 1])
        bg = sb("bg", [P, 1, E1])
        wg_raw = sb("wg_raw", [E1, D])
        wg_t = sb("wg_t", [P, NC, E1])
        w1_raw = sb("w1_raw", [P, NQ, D])
        w1_t = sb("w1_t", [P, NC, NQ * P])
        w2_raw = sb("w2_raw", [P, NC, E1, RANK])
        w2_t = sb("w2_t", [P, NQ, D])
        spread = sb("spread", [E1, NQ * P])
        x_in = sb("x_in", [P, NT, D])
        res = sb("res", [P, NT, D])
        stats, mean_var, small = sb("stats", [P, NT, 6]), sb("mean_var", [P, NT, 2]), sb("small", [P, 4, NT])
        n_tok = sb("n_tok", [P, NT, D])
        n_t = sb("n_t", [P, NC, S])
        tiles = top2_tiles(sb, [sb("top2_space", [P, 31 * NT]), sb("one_hot", [P, 16 * NT])], NT)
        gates = sb("gates", [P, NT, E1])
        gates_t = sb("gates_t", [E1, S])
        hid = sb("hid", [P, NQ, S])
        hid_g = sb("hid_g", [P, NQ, S])
        y_out = sb("y_out", [P, NT, D])

        ps_t = ps("ps_t", [P, 2, S])
        ps_h = ps("ps_h", [P, 2, S])
        ps_e = ps("ps_e", [P, 2, S])
        ps_y = ps("ps_y", [P, 2, S])

        ident_made, const_loaded, gate_made, w_made, w_taken, iota_made, spread_made = (sem(n) for n in (
            "ident_made", "const_loaded", "gate_made", "w_made", "w_taken", "iota_made", "spread_made"))
        x_loaded, res_loaded, chain_sem, stats_made, normed, out_stored = (sem(n) for n in (
            "x_loaded", "res_loaded", "chain", "stats_made", "normed", "out_stored"))
        turned, t_taken, logit_made, logit_taken, gap_made, exp_made, gates_made, gt_made, gt_taken = (sem(n) for n in (
            "turned", "t_taken", "logit_made", "logit_taken", "gap_made", "exp_made", "gates_made", "gt_made", "gt_taken"))
        h_made, gelu_made, e_made, gated, y_made, y_taken = (sem(n) for n in (
            "h_made", "gelu_made", "e_made", "gated", "y_made", "y_taken"))
        NEWTON = 11
        CH = 3 + NEWTON
        TOP = TOP2_STEPS
        N_CONST = 6
        block = stack.enter_context(nc.Block())

        @block.sync
        def _(sp):
            sp.dma_start(x_in[:, :, :], by_token(x_d, 0)).then_inc(x_loaded, 16)
            sp.dma_start(gate[:, :], cfg["gate"].rearrange("(o n) -> o n", o=1).broadcast_to([P, 1])).then_inc(const_loaded, 16)
            sp.dma_start(bg[:, 0, :], cfg["bg"].rearrange("(o n) -> o n", o=1).broadcast_to([P, E1])).then_inc(const_loaded, 16)
            sp.dma_start(wg_raw[:, :], cfg["wg"]).then_inc(const_loaded, 16)
            sp.dma_start(w1_raw[:, :, :], cfg["w1"].rearrange("e r d -> (e r) d").rearrange("(q p) d -> p q d", p=P)
                         ).then_inc(const_loaded, 16)
            for c in range(NC):
                sp.dma_start(w2_raw[:, c], cfg["w2"][:, c * P:c * P + P, :].rearrange("e p r -> p e r")).then_inc(const_loaded, 16)

            def fetch(b):
                sp.wait_ge(normed, NT * b)
                sp.dma_start(x_in[:, :, :], by_token(x_d, b)).then_inc(x_loaded, 16)

            def unit(b, more):
                if more:
                    fetch(b + 1)
                after(sp, y_taken, 2 * b)
                sp.dma_start(res[:, :, :], by_token(x_d, b)).then_inc(res_loaded, 16)
                sp.wait_ge(y_taken, 2 * b + 2)
                sp.dma_start(by_token(out_d, b), y_out[:, :, :]).then_inc(out_stored, 16)

            unit(0, True)
            with sp.Fori(1, B - 1) as b:
                unit(b, True)
            unit(B - 1, False)
            sp.wait_ge(out_stored, 16 * B)

        @block.gpsimd
        def _(pool):
            emit_ident(pool, ident, ident_made)
            for e in range(E1):
                pool.memset(tiles["iota"][:, :, e:e + 1], float(e)).then_inc(iota_made, 1)
            pool.memset(spread[:, :], 1.0).then_inc(spread_made, 1)
            pool.wait_ge(spread_made, 1)
            pool.affine_select(out=spread[:, :], in_=spread[:, :], compare_op=ALU.is_ge, fill=0.0, base=0,
                               pattern=[[1, NQ * P]], channel_multiplier=-RANK).then_inc(spread_made, 1)
            pool.wait_ge(spread_made, 2)
            pool.affine_select(out=spread[:, :], in_=spread[:, :], compare_op=ALU.is_ge, fill=0.0, base=RANK - 1,
                               pattern=[[-1, NQ * P]], channel_multiplier=RANK).then_inc(spread_made, 1)

            def norm(b):
                pool.wait_ge(stats_made, b + 1)
                hold(pool, turned, 2 * b)
                for t in range(NT):
                    pool.tensor_scalar(n_tok[:, t, :], x_in[:, t, :], mean_var[:, t, 0:1], small[:, 1, t:t + 1],
                                       ALU.subtract, ALU.mult).then_inc(normed, 1)
            norm(0)
            with pool.Fori(0, B - 1) as b:
                norm(b + 1)

        @block.tensor
        def _(pe):
            pe.wait_ge(ident_made, 2)
            pe.wait_ge(const_loaded, 16 * N_CONST)
            for c in range(NC):
                for q in range(NQ):
                    last = pe.transpose(ps_h[:, c, q * P:q * P + P], w1_raw[:, q, c * P:c * P + P], ident[:, :])
                last.then_inc(w_made, 1)
            for q in range(NQ):
                for c in range(NC):
                    last = pe.transpose(ps_e[:, q // 2, (q % 2) * D + c * P:(q % 2) * D + c * P + P],
                                        w2_raw[:, c, 2 * q:2 * q + 2, :].rearrange("p e r -> p (e r)"), ident[:, :])
                if q % 2:
                    last.then_inc(w_made, 1)
            for c in range(NC):
                last = pe.transpose(ps_y[:, 0, c * E1:c * E1 + E1], wg_raw[:, c * P:c * P + P], ident[0:E1, 0:E1])
            last.then_inc(w_made, 1)
            pe.wait_ge(w_taken, 5)
            pe.wait_ge(spread_made, 3)

            def turn(b):
                pe.wait_ge(normed, NT * b + NT)
                for c in range(NC):
                    after(pe, t_taken, 2 * b)
                    for t in range(NT):
                        last = pe.transpose(ps_t[:, c, t * P:t * P + P], n_tok[:, t, c * P:c * P + P], ident[:, :])
                    last.then_inc(turned, 1)

            def logits(b):
                pe.wait_ge(t_taken, 2 * b + 2)
                after(pe, gt_taken, b)
                for t in range(NT):
                    for c in range(NC):
                        last = pe.matmul(ps_t[:, 0, t * E1:t * E1 + E1], n_t[:, c, t * P:t * P + P], wg_t[:, c, :],
                                         start=(c == 0), stop=(c == NC - 1))
                last.then_inc(logit_made, 1)

            def turn_gates(b):
                pe.wait_ge(gates_made, b + 1)
                for t in range(NT):
                    last = pe.transpose(ps_t[0:E1, 1, t * P:t * P + P], gates[:, t, :], ident[:, :])
                last.then_inc(gt_made, 1)

            def experts_in(b):
                for q in range(NQ):
                    after(pe, gelu_made, NQ * b + q - 1)
                    for c in range(NC):
                        last = pe.matmul(ps_h[:, q % 2, :], w1_t[:, c, q * P:q * P + P], n_t[:, c, :],
                                         start=(c == 0), stop=(c == NC - 1))
                    last.then_inc(h_made, 1)
                    if q == 0:
                        pe.wait_ge(gt_taken, b + 1)
                    after(pe, gated, NQ * b + q - 1)
                    pe.matmul(ps_e[:, q % 2, :], spread[:, q * P:q * P + P], gates_t[:, :],
                              start=True, stop=True).then_inc(e_made, 1)

            def experts_out(b):
                pe.wait_ge(gated, NQ * b + NQ)
                for t in range(NT):
                    if t % 2 == 0:
                        after(pe, y_taken, 2 * b + t // 2 - 1)
                    for q in range(NQ):
                        last = pe.matmul(ps_y[:, t // 2, (t % 2) * D:(t % 2) * D + D], hid_g[:, q, t * P:t * P + P],
                                         w2_t[:, q, :], start=(q == 0), stop=(q == NQ - 1))
                    if t % 2:
                        last.then_inc(y_made, 1)

            def unit(b, more):
                experts_in(b)
                if more:
                    turn(b + 1)
                    logits(b + 1)
                experts_out(b)
                if more:
                    turn_gates(b + 1)

            turn(0)
            logits(0)
            turn_gates(0)
            unit(0, True)
            with pe.Fori(1, B - 1) as b:
                unit(b, True)
            unit(B - 1, False)

        @block.scalar
        def _(act):
            act.wait_ge(const_loaded, 16 * N_CONST)
            act.activation(gate[:, :], gate[:, :], ACT.Tanh).then_inc(gate_made, 1)

            def take(b):
                for c in range(NC):
                    act.wait_ge(turned, 2 * b + c + 1)
                    if c == 0:
                        after(act, h_made, NQ * b)
                    act.activation(n_t[:, c, :], ps_t[:, c, :], ACT.Copy).then_inc(t_taken, 1)
                act.wait_ge(gap_made, b + 1)
                act.activation(tiles["g"][:, 1, :], tiles["g"][:, 0, :], ACT.Exp).then_inc(exp_made, 1)

            def gelus(b):
                for q in range(NQ):
                    act.wait_ge(h_made, NQ * b + q + 1)
                    after(act, gated, NQ * (b - 1) + q + 1)
                    act.activation(hid[:, q, :], ps_h[:, q % 2, :], ACT.Gelu).then_inc(gelu_made, 1)

            def unit(b, more):
                gelus(b)
                if more:
                    take(b + 1)

            take(0)
            unit(0, True)
            with act.Fori(1, B - 1) as b:
                unit(b, True)
            unit(B - 1, False)

        @block.vector
        def _(dve):
            for c in range(NC):
                dve.wait_ge(w_made, c + 1)
                dve.tensor_copy(w1_t[:, c, :], ps_h[:, c, :]).then_inc(w_taken, 1)
            for k in range(2):
                dve.wait_ge(w_made, k + 3)
                dve.tensor_copy(w2_t[:, 2 * k:2 * k + 2, :].rearrange("p q d -> p (q d)"), ps_e[:, k, :]).then_inc(w_taken, 1)
            dve.wait_ge(w_made, 5)
            dve.tensor_copy(wg_t[:, :, :].rearrange("p c e -> p (c e)"), ps_y[:, 0, 0:NC * E1]).then_inc(w_taken, 1)
            dve.wait_ge(gate_made, 1)
            dve.tensor_scalar(gate2[:, :], gate[:, :], 2.0, None, ALU.mult).then_inc(w_taken, 1)
            dve.wait_ge(w_taken, 6)
            dve.wait_ge(iota_made, E1)

            def stats_of(b):
                step = Chain(dve, chain_sem, (CH + TOP) * b)
                dve.wait_ge(x_loaded, 16 * (b + 1))
                after(dve, normed, NT * b)
                for t in range(NT):
                    last = dve.bn_stats(stats[:, t, :], x_in[:, t, :])
                step(last, hold)
                for t in range(NT):
                    last = dve.bn_aggr(mean_var[:, t, :], stats[:, t, :])
                step(last)
                step(dve.tensor_scalar(small[:, 0, :], mean_var[:, :, 1], EPS, None, ALU.add))
                emit_rsqrt(dve, step, small[:, 1, :], small[:, 0, :], small[:, 2, :])
                dve.sem_inc(stats_made, 1)

            def gating(b):
                step = Chain(dve, chain_sem, (CH + TOP) * b + CH)
                dve.wait_ge(logit_made, b + 1)
                dve.tensor_tensor(tiles["logits"][:, :, :], ps_t[:, 0, 0:NT * E1].rearrange("p (t e) -> p t e", e=E1),
                                  bg[:, :, :].broadcast_to([P, NT, E1]), ALU.add).then_inc(logit_taken, 1)
                hold(dve, logit_taken, b + 1)
                hold(dve, gt_made, b)
                emit_top2(dve, step, tiles, gap_made, exp_made, b, gates[:, :, :])
                dve.sem_inc(gates_made, 1)

            def take_gates(b):
                dve.wait_ge(gt_made, b + 1)
                dve.tensor_copy(gates_t[:, :], ps_t[0:E1, 1, :]).then_inc(gt_taken, 1)

            def unit(b, more):
                if more:
                    stats_of(b + 1)
                for q in range(NQ):
                    dve.wait_ge(e_made, NQ * b + q + 1)
                    dve.wait_ge(gelu_made, NQ * b + q + 1)
                    if q == 0:
                        after(dve, y_made, 2 * b)
                    dve.tensor_tensor(hid_g[:, q, :], hid[:, q, :], ps_e[:, q % 2, :], ALU.mult).then_inc(gated, 1)
                if more:
                    gating(b + 1)
                for k in range(2):
                    dve.wait_ge(y_made, 2 * b + k + 1)
                    dve.wait_ge(res_loaded, 16 * (b + 1))
                    after(dve, out_stored, 16 * b)
                    dve.scalar_tensor_tensor(y_out[:, 2 * k:2 * k + 2, :], ps_y[:, k, :].rearrange("p (t d) -> p t d", d=D),
                                             gate2[:, 0:1], res[:, 2 * k:2 * k + 2, :], ALU.mult, ALU.add).then_inc(y_taken, 1)
                if more:
                    take_gates(b + 1)

            stats_of(0)
            gating(0)
            take_gates(0)
            unit(0, True)
            with dve.Fori(1, B - 1) as b:
                unit(b, True)
            unit(B - 1, False)


_OUTS = [((B, S, D), "float32")]


def build(nc, ins, outs):
    out = outs[0]
    x1, h0, h, x2, x3 = (nc.dram_tensor(name, [B, S, D], F32) for name in ("x1", "h0", "h", "x2", "x3"))

    def cross(layer, x, to, mask):
        w = lambda kind: [ins[f"L{layer}_xattn_{kind}{m}"] for m in "qkvo"]
        build_attention(nc, f"cross{layer}", dict(
            x=x, ctx=ins["ctx_1024"], mask=mask, res=x, out=to, gate=ins["g_xattn"][layer:layer + 1],
            w=w("W"), bias=w("b")))

    stage_sems = range(min(nc.free_semaphores), max(nc.free_semaphores) + 1)

    def next_stage():
        nc.all_engine_barrier(sems_to_clear=stage_sems)

    cross(0, ins["x"], x1, ins["mask_BxS2_bf1"])
    next_stage()
    build_attention(nc, "self", dict(
        x=x1, ctx=None, mask=None, res=h0, out=h, gate=None, w=[ins[f"L0_ffn_w{m}"] for m in "qkvo"],
        ln_w=ins["L0_ffn_ln1_w"]))
    next_stage()
    build_swiglu_moe(nc, "swiglu", dict(
        x=x1, h=h, out=x2, gate=ins["g_ffn"][0:1], ln_w=ins["L0_ffn_ln2_w"], gate_w=ins["L0_ffn_gate_w"],
        w1=ins["L0_ffn_w1"], w2=ins["L0_ffn_w2"], w3=ins["L0_ffn_w3"]))
    next_stage()
    cross(1, x2, x3, None)
    next_stage()
    build_lora_moe(nc, "lora", dict(
        x=x3, out=out, gate=ins["g_ffn"][1:2], wg=ins["L1_ffn_Wg"], bg=ins["L1_ffn_bg"],
        w1=ins["L1_ffn_W1"], w2=ins["L1_ffn_W2"]))


def kernel(**inputs):
    import numpy as np
    import concourse.bacc as bacc
    from concourse.bass_utils import run_bass_kernel_spmd

    nc = bacc.Bacc("TRN2", target_bir_lowering=False, num_devices=1)
    arrays, ins = {}, {}
    for name, value in inputs.items():
        value = np.ascontiguousarray(np.asarray(value))
        dt = U8 if value.dtype == np.bool_ else mybir.dt.from_np(value.dtype)
        arrays[f"in_{name}_dram"] = value
        ins[name] = nc.dram_tensor(f"in_{name}_dram", value.shape, dt, kind="ExternalInput").ap()
    outs = [nc.dram_tensor(f"out_{i}_dram", shape, mybir.dt.from_np(np.dtype(dtype)), kind="ExternalOutput").ap()
            for i, (shape, dtype) in enumerate(_OUTS)]
    build(nc, ins, outs)
    result = run_bass_kernel_spmd(nc, [arrays], core_ids=[0])
    return result.results[0]["out_0_dram"]
```
